# Optimizing a Trainium2 kernel written in Bass

```python
import numpy as np
import jax
import jax.numpy as jnp

def _softmax(x, axis=-1):
    return jax.nn.softmax(x, axis=axis)

def _gelu(x):
    return jax.nn.gelu(x, approximate=True)

def _silu(x):
    return jax.nn.silu(x)

def _sigmoid(x):
    return jax.nn.sigmoid(x)

def _layernorm(x, axis=-1, eps=1e-05):
    m = jnp.mean(x, axis=axis, keepdims=True)
    v = jnp.var(x, axis=axis, keepdims=True)
    return (x - m) / jnp.sqrt(v + eps)

def _scatter_add(tgt, idx, src, axis=0):
    return tgt.at[idx].add(src)

def _segment_sum(src, seg, n):
    return jax.ops.segment_sum(src, seg, n)
kernel_name = 'mk_decoder_preln_d1_seqx_r8_a4549b'

def setup_inputs(seed: int=0):
    np.random.seed(seed)
    _w = jnp.asarray

    def _rec_inputs():
        import jax
        import jax.numpy as jnp
        _rk = jax.random.key(seed)
        x = 7.22e-05 + 1 * jax.random.normal(jax.random.fold_in(_rk, 1), (4, 512, 128), jnp.float32)
        _lenS = 512 - jax.random.randint(jax.random.fold_in(_rk, 7), (4,), 0, max(1, 512 // 4) + 1, jnp.int32)
        _lenS2 = 32 - jax.random.randint(jax.random.fold_in(_rk, 8), (4,), 0, max(1, 32 // 4) + 1, jnp.int32)
        _ctx_768P = jax.random.normal(jax.random.fold_in(_rk, 11), (4, 16, 96), jnp.float32)
        _ctx_768c = jax.random.dirichlet(jax.random.fold_in(_rk, 511), 0.3 * jnp.ones((16,), jnp.float32), (4, 32))
        _ctx_768t = jnp.einsum('bsk,bkd->bsd', _ctx_768c, _ctx_768P)
        _ctx_768t = _ctx_768t * jax.lax.rsqrt(jnp.mean(jnp.square(_ctx_768t)) + 1e-12) * 0.953939
        ctx_768 = -0.000191848 + 0.999787 * (_ctx_768t + 0.3 * jax.random.normal(jax.random.fold_in(_rk, 611), (4, 32, 96), jnp.float32))
        return (x, ctx_768)
    x, ctx_768 = _rec_inputs()

    def _L0_attn_setup():
        import jax, jax.numpy as jnp
        import numpy as np
        import math
        N_HEAD = 16
        HEAD_DIM = 64
        N_EMBD = 128
        MIN_CTX = 32
        FULL_CTX = 128

        def _pruning_ratio(T):
            if T < MIN_CTX:
                return 1.0
            if T >= FULL_CTX:
                return 0.2
            progress = (T - MIN_CTX) / (FULL_CTX - MIN_CTX)
            return 0.5 - 0.3 * progress
        key = jax.random.key(seed)
        k1, k2, k3, k4, k5 = jax.random.split(key, 5)
        B, T = (1, 256)
        x = jax.random.normal(k1, (B, T, N_EMBD), dtype=jnp.float32)
        W_attn = jax.random.normal(k2, (3 * N_HEAD * HEAD_DIM, N_EMBD), dtype=jnp.float32) * 0.02
        b_attn = jnp.zeros((3 * N_HEAD * HEAD_DIM,), dtype=jnp.float32)
        W_proj = jax.random.normal(k3, (N_EMBD, N_HEAD * HEAD_DIM), dtype=jnp.float32) * 0.02
        b_proj = jnp.zeros((N_EMBD,), dtype=jnp.float32)
        return {'x': x, 'W_attn': W_attn, 'b_attn': b_attn, 'W_proj': W_proj, 'b_proj': b_proj}
    _L0_attn_all = _L0_attn_setup()
    _L0_attn_in = {k: v for k, v in _L0_attn_all.items() if k in ('W_attn', 'b_attn', 'W_proj', 'b_proj')}
    del _L0_attn_all

    def _L0_xattn_setup():
        import jax, jax.numpy as jnp
        import numpy as np
        DIM_Q = 128
        DIM_KV = 96
        N_HEADS = 4

        def _split_heads(x):
            b, l, d = x.shape
            return x.reshape(b, l, N_HEADS, d // N_HEADS).transpose(0, 2, 1, 3)
        key = jax.random.key(seed)
        ks = jax.random.split(key, 7)
        b, lq, lkv = (4, 256, 256)
        q = jax.random.normal(ks[0], (b, lq, DIM_Q), dtype=jnp.float32)
        kv = jax.random.normal(ks[1], (b, lkv, DIM_KV), dtype=jnp.float32)
        s_q = 1.0 / np.sqrt(DIM_Q)
        s_kv = 1.0 / np.sqrt(DIM_KV)
        Wq = jax.random.normal(ks[2], (DIM_Q, DIM_Q), dtype=jnp.float32) * s_q
        Wk = jax.random.normal(ks[3], (DIM_Q, DIM_KV), dtype=jnp.float32) * s_kv
        Wv = jax.random.normal(ks[4], (DIM_Q, DIM_KV), dtype=jnp.float32) * s_kv
        Wo = jax.random.normal(ks[5], (DIM_Q, DIM_Q), dtype=jnp.float32) * s_q
        bo = jax.random.normal(ks[6], (DIM_Q,), dtype=jnp.float32) * 0.01
        return {'q': q, 'kv': kv, 'Wq': Wq, 'Wk': Wk, 'Wv': Wv, 'Wo': Wo, 'bo': bo}
    _L0_xattn_all = _L0_xattn_setup()
    _L0_xattn_in = {k: v for k, v in _L0_xattn_all.items() if k in ('Wq', 'Wk', 'Wv', 'Wo', 'bo')}
    del _L0_xattn_all

    def _L0_ffn_setup():
        import jax, jax.numpy as jnp
        import numpy as np
        LN_EPS = 1e-12
        key = jax.random.key(seed)
        ks = jax.random.split(key, 8)
        B, S, H, I, E = (4, 256, 128, 512, 8)
        sH = 1.0 / np.sqrt(H)
        sI = 1.0 / np.sqrt(I)
        return {'hidden_states': jax.random.normal(ks[0], (B, S, H), dtype=jnp.float32), 'Wr': jax.random.uniform(ks[1], (E, H), jnp.float32, -sH, sH), 'W1': jax.random.uniform(ks[2], (E, H, I), jnp.float32, -sH, sH), 'b1': jax.random.uniform(ks[3], (E, I), jnp.float32, -sH, sH), 'Wo': jax.random.uniform(ks[4], (I, H), jnp.float32, -sI, sI), 'bo': jax.random.uniform(ks[5], (H,), jnp.float32, -sI, sI), 'gamma': jnp.ones((H,), jnp.float32), 'beta': jnp.zeros((H,), jnp.float32)}
    _L0_ffn_all = _L0_ffn_setup()
    _L0_ffn_in = {k: v for k, v in _L0_ffn_all.items() if k in ('Wr', 'W1', 'b1', 'Wo', 'bo', 'gamma', 'beta')}
    del _L0_ffn_all
    return {'x': x, 'ctx_768': ctx_768, 'L0_attn_W_attn': _L0_attn_in['W_attn'], 'L0_attn_b_attn': _L0_attn_in['b_attn'], 'L0_attn_W_proj': _L0_attn_in['W_proj'], 'L0_attn_b_proj': _L0_attn_in['b_proj'], 'L0_xattn_Wq': _L0_xattn_in['Wq'], 'L0_xattn_Wk': _L0_xattn_in['Wk'], 'L0_xattn_Wv': _L0_xattn_in['Wv'], 'L0_xattn_Wo': _L0_xattn_in['Wo'], 'L0_xattn_bo': _L0_xattn_in['bo'], 'L0_ffn_Wr': _L0_ffn_in['Wr'], 'L0_ffn_W1': _L0_ffn_in['W1'], 'L0_ffn_b1': _L0_ffn_in['b1'], 'L0_ffn_Wo': _L0_ffn_in['Wo'], 'L0_ffn_bo': _L0_ffn_in['bo'], 'L0_ffn_gamma': _L0_ffn_in['gamma'], 'L0_ffn_beta': _L0_ffn_in['beta']}

def reference(x, ctx_768, L0_attn_W_attn, L0_attn_b_attn, L0_attn_W_proj, L0_attn_b_proj, L0_xattn_Wq, L0_xattn_Wk, L0_xattn_Wv, L0_xattn_Wo, L0_xattn_bo, L0_ffn_Wr, L0_ffn_W1, L0_ffn_b1, L0_ffn_Wo, L0_ffn_bo, L0_ffn_gamma, L0_ffn_beta):
    import jax
    import jax.numpy as jnp

    def _L0_attn_ref(x, W_attn, b_attn, W_proj, b_proj):
        import jax, jax.numpy as jnp
        import numpy as np
        import math
        N_HEAD = 16
        HEAD_DIM = 64
        N_EMBD = 128
        MIN_CTX = 32
        FULL_CTX = 128

        def _pruning_ratio(T):
            if T < MIN_CTX:
                return 1.0
            if T >= FULL_CTX:
                return 0.2
            progress = (T - MIN_CTX) / (FULL_CTX - MIN_CTX)
            return 0.5 - 0.3 * progress
        B, T, C = x.shape
        H, hd = (N_HEAD, HEAD_DIM)
        qkv = x @ W_attn.T + b_attn
        q, k, v = jnp.split(qkv, 3, axis=-1)
        q = q.reshape(B, T, H, hd).transpose(0, 2, 1, 3)
        k = k.reshape(B, T, H, hd).transpose(0, 2, 1, 3)
        v = v.reshape(B, T, H, hd).transpose(0, 2, 1, 3)
        att = jnp.einsum('bhqd,bhkd->bhqk', q, k) * (1.0 / math.sqrt(hd))
        i = jnp.arange(T)
        causal = i[None, :] <= i[:, None]
        neg_inf = jnp.float32(-jnp.inf)
        att = jnp.where(causal[None, None], att, neg_inf)
        S = jnp.maximum(att[:, 0], 0.0)
        keepS = (i[None, :] != 0) & (i[:, None] != i[None, :])
        S = jnp.where(keepS[None], S, 0.0)
        S_shifted = jnp.roll(S, 1, axis=-2).at[:, 0, :].set(0.0)
        FF = jnp.cumsum(S_shifted, axis=-2)
        att = att - FF[:, None]
        ratio = _pruning_ratio(T)
        memory_budget = max(1, int(T * ratio))
        if ratio < 1.0:
            FF_mod = jnp.where(causal[None], FF, jnp.inf)
            sorted_idx = jnp.argsort(FF_mod, axis=-1)
            eff_k = jnp.minimum(memory_budget - 1, i + 1)
            sel = i[None, :] < eff_k[:, None]
            keep = jnp.zeros((B, T, T), dtype=bool)
            keep = keep.at[jnp.arange(B)[:, None, None], i[None, :, None], sorted_idx].set(jnp.broadcast_to(sel[None], (B, T, T)))
            keep = keep | jnp.eye(T, dtype=bool)[None]
            att = jnp.where(keep[:, None], att, neg_inf)
        y = jax.nn.softmax(att, axis=-1) @ v
        y = y.transpose(0, 2, 1, 3).reshape(B, T, H * hd)
        y = y @ W_proj.T + b_proj
        return y

    def _L0_xattn_ref(q, kv, Wq, Wk, Wv, Wo, bo):
        import jax, jax.numpy as jnp
        import numpy as np
        DIM_Q = 128
        DIM_KV = 96
        N_HEADS = 4

        def _split_heads(x):
            b, l, d = x.shape
            return x.reshape(b, l, N_HEADS, d // N_HEADS).transpose(0, 2, 1, 3)
        qp = q @ Wq.T
        kp = kv @ Wk.T
        vp = kv @ Wv.T
        qh, kh, vh = (_split_heads(qp), _split_heads(kp), _split_heads(vp))
        scale = (DIM_Q // N_HEADS) ** (-0.5)
        scores = jnp.einsum('bhqd,bhkd->bhqk', qh, kh) * scale
        attn = jax.nn.softmax(scores, axis=-1)
        ctx = jnp.einsum('bhqk,bhkd->bhqd', attn, vh)
        b, h, lq, hd = ctx.shape
        ctx = ctx.transpose(0, 2, 1, 3).reshape(b, lq, h * hd)
        return ctx @ Wo.T + bo

    def _L0_ffn_ref(hidden_states, Wr, W1, b1, Wo, bo, gamma, beta):
        import jax, jax.numpy as jnp
        import numpy as np
        LN_EPS = 1e-12
        B, S, H = hidden_states.shape
        E = Wr.shape[0]
        x = hidden_states.reshape(-1, H)
        router_logits = x @ Wr.T
        expert_idx = jnp.argmax(jax.nn.softmax(router_logits, axis=-1), axis=-1)
        inter = jnp.zeros((x.shape[0], W1.shape[2]), dtype=x.dtype)
        for e in range(E):
            mask = (expert_idx == e)[:, None].astype(x.dtype)
            inter = inter + mask * jax.nn.gelu(x @ W1[e] + b1[e], approximate=False)
        y = inter @ Wo + bo + x
        mu = jnp.mean(y, axis=-1, keepdims=True)
        var = jnp.mean(jnp.square(y - mu), axis=-1, keepdims=True)
        out = (y - mu) * jax.lax.rsqrt(var + LN_EPS) * gamma + beta
        return out.reshape(B, S, H)
    x = x + _L0_attn_ref(_layernorm(x, axis=-1), L0_attn_W_attn, L0_attn_b_attn, L0_attn_W_proj, L0_attn_b_proj)
    x = x + _L0_xattn_ref(_layernorm(x, axis=-1), ctx_768, L0_xattn_Wq, L0_xattn_Wk, L0_xattn_Wv, L0_xattn_Wo, L0_xattn_bo)
    x = x + _L0_ffn_ref(_layernorm(x, axis=-1), L0_ffn_Wr, L0_ffn_W1, L0_ffn_b1, L0_ffn_Wo, L0_ffn_bo, L0_ffn_gamma, L0_ffn_beta)
    return x

_drawn_inputs = setup_inputs


def setup_inputs(seed=0):
    import zlib

    import numpy as np

    out = dict(_drawn_inputs(seed))
    spreads = {'L0_attn_b_attn': (0.0, 0.1),
     'L0_attn_b_proj': (0.0, 0.1),
     'L0_ffn_gamma': (1.0, 0.2),
     'L0_ffn_beta': (0.0, 0.1)}
    factors = {'L0_xattn_bo': 3.938, 'L0_ffn_b1': 6.609, 'L0_ffn_bo': 4.277}
    for name, (base, spread) in spreads.items():
        noise = np.random.default_rng([zlib.crc32(name.encode()), seed]).standard_normal(out[name].shape)
        drawn = base * np.exp(spread * noise) if base else spread * noise
        out[name] = jnp.asarray(drawn.astype(out[name].dtype))
    for name, factor in factors.items():
        out[name] = (out[name] * factor).astype(out[name].dtype)
    return out
```

```python
from contextlib import ExitStack

import concourse.bass as bass
from concourse import mybir

F32 = mybir.dt.float32
ALU = mybir.AluOpType
ACT = mybir.ActivationFunctionType
AX = mybir.AxisListType

P = 128
B, T, C = 4, 512, 128
NT = T // P
H, HD = 16, 64
D = H * HD
PAIRS = H // 2
QUAD = 4
QUADS = H // QUAD
XH, XKV, CD = 4, 32, 96
XHD = C // XH
E, FF = 8, 512
NF = FF // P
W = [(t + 1) * P for t in range(NT)]
QOFF = [sum(W[:t]) for t in range(NT)]
CAUSAL = sum(W)
KOFF = [0, T, 2 * T, 2 * T - P]
BUDGET = max(1, int(T * 0.2))
KEPT = BUDGET - 1
ROUNDS = -(-KEPT // 8)
PADS = ROUNDS * 8 - KEPT
WOFF = [QOFF[t] + PADS * t for t in range(NT)]
BIG = 1.0e30
PAD = 2.0e30
MARK = -3.0e38
LN_EPS, FFN_EPS = 1e-5, 1e-12


def program(nc, a, out):
    with ExitStack() as ctx:
        def sb(name, shape, dt=F32):
            return ctx.enter_context(nc.sbuf_tensor(name, shape, dt))

        def sem(name):
            return ctx.enter_context(nc.semaphore(name))

        bank = [ctx.enter_context(nc.psum_tensor(f"bank{i}", [P, 512], F32)) for i in range(8)]

        ident = sb("ident", [P, P])
        ones = sb("ones", [P, P])
        before = sb("before", [P, P])
        halfpow = sb("halfpow", [P, NT])
        sel = sb("sel", [E, E, P])
        rank = sb("rank", [P, NT, E])
        w_in = sb("w_in", [P, 3 * D])
        b_in = sb("b_in", [P, 3 * PAIRS])
        bq_neg = sb("bq_neg", [P, PAIRS])
        w_proj = sb("w_proj", [P, PAIRS, C])
        xwq = sb("xwq", [C, C])
        xwk = sb("xwk", [CD, C])
        xwv = sb("xwv", [CD, C])
        xwo = sb("xwo", [C, C])
        ctxT = sb("ctxT", [CD, B, XKV])
        ctx4 = sb("ctx4", [CD, XH, XKV])
        w_r = sb("w_r", [C, E])
        w1 = sb("w1", [C, E, FF])
        b1 = sb("b1", [E, FF])
        w2 = sb("w2", [P, NF, C])
        rows = sb("rows", [1, 5, C])
        wide = sb("wide", [P, 5, C])

        x = sb("x", [P, B * NT, C])
        xnT_all = sb("xnT_all", [C, B * T])
        xn = sb("xn", [P, NT, C])
        xnT = sb("xnT", [C, T])
        stats = sb("stats", [P, NT, 6])
        mv = sb("mv", [P, NT, 2])
        rstd = sb("rstd", [P, NT])
        q0T = sb("q0T", [HD, T])
        k0T = sb("k0T", [HD, T])
        F_all = sb("F_all", [P, B * CAUSAL])
        work = sb("work", [P, CAUSAL + PADS * NT])
        best = sb("best", [P, NT, 8])
        bias = sb("bias", [P, CAUSAL])
        wblk = [sb(f"wblk{i}", [C, 2, P]) for i in range(2)]
        bblk = [sb(f"bblk{i}", [P, 2]) for i in range(2)]
        qT = [sb(f"qT{i}", [P, T]) for i in range(2)]
        kT = [sb(f"kT{i}", [P, T]) for i in range(2)]
        V = sb("V", [P, NT, D])
        neg = [sb(f"neg{i}", [P, CAUSAL]) for i in range(2)]
        low = [sb(f"low{i}", [P, NT]) for i in range(2)]
        prob = [sb(f"prob{i}", [P, CAUSAL]) for i in range(2)]
        total = [sb(f"total{i}", [P, NT]) for i in range(2)]
        inv = [sb(f"inv{i}", [P, NT]) for i in range(2)]
        probT = sb("probT", [P, 3 * T])
        S0, F0 = neg[0], prob[0]
        y = sb("y", [P, NT, D])
        y_flat = y[:, :, :].rearrange("p t d -> p (t d)")
        interT = y_flat[:, 0:NF * T].rearrange("p (i q) -> p i q", i=NF)
        bv_wide = y_flat[:, 0:PAIRS * P].rearrange("p (c q) -> p c q", c=PAIRS)
        share = sb("share", [P, PAIRS * T])
        yT = share[:, :].rearrange("p (c q) -> p c q", c=PAIRS)
        xm = share[:, :].rearrange("p (e q) -> p e q", e=E)
        kblk = sb("kblk", [P, P])
        vblk = sb("vblk", [P, P])
        xkT = sb("xkT", [C, B * XKV])
        xqT = sb("xqT", [C, T])
        xs = sb("xs", [P, NT * XH, XKV])
        xmax = sb("xmax", [P, NT * XH])
        xsum = sb("xsum", [P, NT * XH])
        xpT = sb("xpT", [P, T])
        xcT = xqT
        hnT = sb("hnT", [C, T])
        lg = sb("lg", [P, NT, E])
        lmax = sb("lmax", [P, NT])
        pick = sb("pick", [P, NT, E])
        maskT = sb("maskT", [E, T])
        res = sb("res", [P, NT, C])

        lsum = sb("lsum", [P, NT])
        r = sb("r", [P, NT, C])
        eps = sb("eps", [P, 2])

        loads = sem("loads")
        stored = sem("stored")
        pool_own = sem("pool_own")
        dve_own = sem("dve_own")
        pick_own = [sem(f"pick_own{t}") for t in range(NT)]
        const_pe = sem("const_pe")
        const_dve = sem("const_dve")
        wide_ready = sem("wide_ready")
        act_own = sem("act_own")
        wide_mm = sem("wide_mm")
        xk_mm = sem("xk_mm")
        xk_ready = sem("xk_ready")
        var_ready = sem("var_ready")
        rstd_ready = sem("rstd_ready")
        xn_ready = sem("xn_ready")
        xnT_mm = sem("xnT_mm")
        xnT_evac = sem("xnT_evac")
        xnT_keep = sem("xnT_keep")
        xnT_kept = sem("xnT_kept")
        h0_mm = sem("h0_mm")
        h0_ready = sem("h0_ready")
        s0_mm = sem("s0_mm")
        s0_relu = sem("s0_relu")
        s0_ready = sem("s0_ready")
        ff_mm = sem("ff_mm")
        ff_read = sem("ff_read")
        f0_free = sem("f0_free")
        work_ready = sem("work_ready")
        picked = sem("picked")
        bias_ready = sem("bias_ready")
        xT_ready = sem("xT_ready")
        w_ready = sem("w_ready")
        v_mm = sem("v_mm")
        v_read = sem("v_read")
        qk_mm = sem("qk_mm")
        qk_ready = sem("qk_ready")
        score_mm = sem("score_mm")
        neg_ready = sem("neg_ready")
        exp_done = sem("exp_done")
        tr_mm = sem("tr_mm")
        tr_read = sem("tr_read")
        pv_mm = sem("pv_mm")
        o_free = sem("o_free")
        head_done = sem("head_done")
        vx_ready = sem("vx_ready")
        vx_mm = sem("vx_mm")
        vblk_ready = sem("vblk_ready")
        kblk_ready = sem("kblk_ready")
        yT_mm = [sem("yT_mm_act"), sem("yT_mm_dve")]
        yT_read = [sem("yT_read_act"), sem("yT_read_dve")]
        proj_mm = sem("proj_mm")
        xq_mm = sem("xq_mm")
        xq_read = sem("xq_read")
        xs_mm = sem("xs_mm")
        xs_ready = sem("xs_ready")
        xs_exp = sem("xs_exp")
        xp_ready = sem("xp_ready")
        xp_mm = sem("xp_mm")
        xp_read = sem("xp_read")
        xc_mm = sem("xc_mm")
        xc_read = sem("xc_read")
        xo_mm = sem("xo_mm")
        lg_mm = sem("lg_mm")
        lg_ready = sem("lg_ready")
        lg_exp = sem("lg_exp")
        pick_ready = sem("pick_ready")
        mask_mm = sem("mask_mm")
        mask_read = sem("mask_read")
        bc_mm = sem("bc_mm")
        xm_ready = sem("xm_ready")
        up_mm = sem("up_mm")
        gelu_done = sem("gelu_done")
        down_mm = sem("down_mm")
        res_ready = sem("res_ready")
        res_free = sem("res_free")

        def tok(t):
            return slice(t * P, (t + 1) * P)

        def tile(buf, t, off=QOFF):
            return buf[:, off[t]:off[t] + W[t]]

        def diag(buf, t):
            return buf[:, QOFF[t] + t * P:QOFF[t] + W[t]]

        SCORE = [bank[0][:, 0:W[0]], bank[0][:, W[0]:W[0] + W[1]], bank[1][:, 0:W[2]], bank[2][:, 0:W[3]]]

        def probT_tile(k, t):
            return probT[:, KOFF[k] + (t - k) * P:KOFF[k] + (t - k + 1) * P]

        LOADS = [
            (x[:, :, :], a["x"]), (w_in[:, :], a["w_in"]), (b_in[:, :], a["b_in"]),
            (w_proj[:, :, :], a["w_proj"]), (xwq[:, :], a["xwq"]), (xwk[:, :], a["xwk"]),
            (xwv[:, :], a["xwv"]), (xwo[:, :], a["xwo"]), (ctxT[:, :, :], a["ctxT"]),
            (w_r[:, :], a["w_r"]), (w1[:, :, :], a["w1"]), (b1[:, :], a["b1"]),
            (w2[:, :, :], a["w2"]), (rows[:, :, :], a["rows"]),
        ]

        block = ctx.enter_context(nc.Block())

        @block.sync
        def _(sp):
            for dst, src in LOADS:
                sp.dma_start(dst, src).then_inc(loads, 16)
            sp.sem_inc(res_free, 1)
            with sp.Fori(0, B) as b:
                sp.wait_ge(res_ready, 1)
                sp.sem_inc(res_ready, -1)
                sp.dma_start(out[bass.ds(b, 1), :, :].rearrange("o (t p) c -> p (o t) c", p=P),
                             res[:, :, :]).then_inc(stored, 16)
                sp.wait_ge(stored, 16)
                sp.sem_inc(stored, -16)
                sp.sem_inc(res_free, 1)

        @block.gpsimd
        def _(pool):
            def own(ins):
                ins.then_inc(pool_own, 1)
                pool.wait_ge(pool_own, 1)
                pool.sem_inc(pool_own, -1)

            def power(eps_col):
                pool.wait_ge(var_ready, 1)
                pool.sem_inc(var_ready, -1)
                own(nc.gpsimd.tensor_scalar(rstd[:, :], mv[:, :, 1], eps_col, None, ALU.add))
                nc.gpsimd.tensor_tensor(rstd[:, :], rstd[:, :], halfpow[:, :], ALU.pow).then_inc(rstd_ready, 1)

            own(nc.gpsimd.memset(ones[:, :], 1.0))
            nc.gpsimd.memset(halfpow[:, :], -0.5)
            for e in range(E):
                nc.gpsimd.memset(rank[:, :, e:e + 1], float(E - e))
            for t in range(NT):
                nc.gpsimd.memset(work[:, WOFF[t]:WOFF[t] + PADS], PAD)
            nc.gpsimd.affine_select(out=ident[:, :], in_=ones[:, :], compare_op=ALU.is_equal, fill=0.0, base=0,
                                    pattern=[[-1, P]], channel_multiplier=1)
            nc.gpsimd.affine_select(out=before[:, :], in_=ones[:, :], compare_op=ALU.is_gt, fill=0.0, base=0,
                                    pattern=[[1, P]], channel_multiplier=-1)
            own(nc.gpsimd.memset(sel[:, :, :], 1.0))
            nc.gpsimd.affine_select(out=sel[:, :, :], in_=sel[:, :, :], compare_op=ALU.is_equal, fill=0.0, base=0,
                                    pattern=[[-1, E], [0, P]], channel_multiplier=1)
            nc.gpsimd.memset(kblk[:, :], 0.0)
            own(nc.gpsimd.memset(vblk[:, :], 0.0))
            pool.sem_inc(const_pe, 1)
            pool.sem_inc(const_dve, 1)
            pool.wait_ge(loads, 16 * len(LOADS))

            with pool.Fori(0, B) as b:
                power(LN_EPS)
                pool.wait_ge(xnT_keep, 1)
                pool.sem_inc(xnT_keep, -1)
                nc.gpsimd.tensor_copy(xnT_all[:, bass.ds(b * T, T)], xnT[:, :]).then_inc(xnT_kept, 1)
                pool.wait_ge(s0_relu, 1)
                pool.sem_inc(s0_relu, -1)
                for t in range(NT):
                    last = nc.gpsimd.affine_select(out=diag(S0, t), in_=diag(S0, t), compare_op=ALU.is_gt,
                                                   fill=0.0, base=0, pattern=[[-1, P]], channel_multiplier=1)
                own(last)
                for t in range(NT):
                    last = nc.gpsimd.memset(S0[:, QOFF[t]:QOFF[t] + 1], 0.0)
                last.then_inc(s0_ready, 1)
                pool.wait_ge(ff_read, 1)
                pool.sem_inc(ff_read, -1)
                for t in range(NT):
                    last = nc.gpsimd.affine_select(out=diag(F0, t), in_=diag(F0, t), compare_op=ALU.is_ge,
                                                   fill=-BIG, base=0, pattern=[[-1, P]], channel_multiplier=1)
                own(last)
                nc.gpsimd.tensor_copy(F_all[:, bass.ds(b * CAUSAL, CAUSAL)], F0[:, :]).then_inc(f0_free, 1)

            def fill_work(b):
                for t in range(NT):
                    last = nc.gpsimd.tensor_copy(work[:, WOFF[t] + PADS:WOFF[t] + PADS + W[t]],
                                                 F_all[:, bass.ds(b * CAUSAL + QOFF[t], W[t])])
                last.then_inc(work_ready, 1)

            def pads():
                for t in range(NT):
                    nc.gpsimd.memset(work[:, WOFF[t]:WOFF[t] + PADS], PAD)

            def make_bias(b):
                pool.wait_ge(picked, 1)
                pool.sem_inc(picked, -1)
                for t in range(NT):
                    own(nc.gpsimd.tensor_scalar(tile(bias, t), work[:, WOFF[t] + PADS:WOFF[t] + PADS + W[t]],
                                                -PAD, BIG, ALU.is_gt, ALU.mult))
                    own(nc.gpsimd.affine_select(out=diag(bias, t), in_=diag(bias, t), compare_op=ALU.not_equal,
                                                fill=0.0, base=0, pattern=[[-1, P]], channel_multiplier=1))
                    last = nc.gpsimd.tensor_tensor(tile(bias, t), tile(bias, t),
                                                   F_all[:, bass.ds(b * CAUSAL + QOFF[t], W[t])], ALU.subtract)
                last.then_inc(bias_ready, 1)

            def fill_weights(i, pair):
                nc.gpsimd.tensor_copy(wblk[i][:, 0, :], w_in[:, bass.ds(pair * P, P)])
                nc.gpsimd.tensor_copy(bblk[i][:, 0:1], bq_neg[:, bass.ds(pair, 1)])
                nc.gpsimd.tensor_copy(bblk[i][:, 1:2], b_in[:, bass.ds(pair + PAIRS, 1)])
                nc.gpsimd.tensor_copy(wblk[i][:, 1, :], w_in[:, bass.ds(pair * P + D, P)]).then_inc(w_ready, 1)

            fill_work(0)
            with pool.Fori(0, B) as b:
                nc.gpsimd.tensor_copy(xnT[:, :], xnT_all[:, bass.ds(b * T, T)]).then_inc(xT_ready, 1)
                for i in range(2):
                    fill_weights(i, i)
                make_bias(b)
                pads()
                fill_work((b + 1) % B)
                for h in range(XH):
                    last = nc.gpsimd.tensor_copy(ctx4[:, h, :], ctxT[:, bass.ds(b, 1), :].rearrange("p o k -> p (o k)"))
                last.then_inc(vx_ready, 1)
                with pool.Fori(0, QUADS - 1) as q:
                    pool.wait_ge(head_done, 1)
                    pool.sem_inc(head_done, -1)
                    fill_weights(0, q * 2 + 2)
                    pool.wait_ge(head_done, 2)
                    pool.sem_inc(head_done, -2)
                    fill_weights(1, q * 2 + 3)
                    pool.wait_ge(head_done, 1)
                    pool.sem_inc(head_done, -1)
                pool.wait_ge(head_done, QUAD)
                pool.sem_inc(head_done, -QUAD)
                for e in (LN_EPS, LN_EPS, FFN_EPS):
                    power(e)

        @block.scalar
        def _(act):
            act.wait_ge(loads, 16 * len(LOADS))
            nc.scalar.activation(bq_neg[:, :], b_in[:, 0:PAIRS], ACT.Copy, scale=-0.125).then_inc(act_own, 1)
            act.wait_ge(act_own, 1)
            act.sem_inc(act_own, -1)
            act.wait_ge(wide_mm, 1)
            act.sem_inc(wide_mm, -1)
            for i in range(5):
                nc.scalar.copy(wide[:, i, :], bank[i][:, 0:C])
            act.wait_ge(xk_mm, 1)
            act.sem_inc(xk_mm, -1)
            nc.scalar.copy(xkT[:, :], bank[5][:, 0:B * XKV]).then_inc(xk_ready, 1)

            def from_bank(dst, src, got, read):
                act.wait_ge(got, 1)
                act.sem_inc(got, -1)
                nc.scalar.copy(dst, src).then_inc(read, 1)

            act.sem_inc(xnT_kept, 1)
            act.sem_inc(f0_free, 1)
            with act.Fori(0, B) as b:
                act.wait_ge(xnT_kept, 1)
                act.sem_inc(xnT_kept, -1)
                from_bank(xnT[:, :], bank[7][:, :], xnT_mm, xnT_evac)
                act.wait_ge(h0_mm, 1)
                act.sem_inc(h0_mm, -1)
                nc.scalar.activation(q0T[:, :], bank[6][0:HD, :], ACT.Identity, scale=-0.125, bias=bq_neg[0:HD, 0:1])
                nc.scalar.activation(k0T[:, :], bank[5][0:HD, :], ACT.Identity, bias=b_in[0:HD, PAIRS:PAIRS + 1])\
                    .then_inc(h0_ready, 1)
                act.wait_ge(s0_mm, 1)
                act.sem_inc(s0_mm, -1)
                for t in range(NT):
                    last = nc.scalar.activation(tile(S0, t), SCORE[t], ACT.Relu, scale=-1.0)
                last.then_inc(s0_relu, 1)
                act.wait_ge(ff_mm, 1)
                act.sem_inc(ff_mm, -1)
                act.wait_ge(f0_free, 1)
                act.sem_inc(f0_free, -1)
                nc.scalar.activation(F0[:, 0:QOFF[2]], bank[3][:, 0:QOFF[2]], ACT.Copy, scale=-1.0)
                nc.scalar.activation(tile(F0, 2), bank[4][:, 0:W[2]], ACT.Copy, scale=-1.0)
                nc.scalar.activation(tile(F0, 3), bank[5][:, 0:W[3]], ACT.Copy, scale=-1.0).then_inc(ff_read, 1)

            def qk_evac(i):
                act.wait_ge(qk_mm, 1)
                act.sem_inc(qk_mm, -1)
                nc.scalar.activation(qT[i][:, :], bank[7][:, :], ACT.Identity, scale=-0.125, bias=bblk[i][:, 0:1])\
                    .then_inc(qk_ready, 1)
                act.wait_ge(qk_mm, 1)
                act.sem_inc(qk_mm, -1)
                nc.scalar.activation(kT[i][:, :], bank[7][:, :], ACT.Identity, bias=bblk[i][:, 1:2])\
                    .then_inc(qk_ready, 1)

            def exps(s):
                for t in range(NT):
                    act.wait_ge(neg_ready, 1)
                    act.sem_inc(neg_ready, -1)
                    nc.scalar.activation(tile(prob[s], t), tile(neg[s], t), ACT.Exp, scale=-1.0,
                                         bias=low[s][:, t:t + 1], accum_out=total[s][:, t:t + 1]).then_inc(exp_done, 1)

            def probT_evac():
                for i, n in ((0, T), (2, T // 2), (1, T)):
                    act.wait_ge(tr_mm, 1)
                    act.sem_inc(tr_mm, -1)
                    nc.scalar.copy(probT[:, i * T:i * T + n], bank[3 + i][:, 0:n]).then_inc(tr_read, 1)

            def quad(last):
                for i in range(QUAD):
                    probT_evac()
                    if not (last and i == QUAD - 1):
                        exps((i + 1) % 2)
                    if i == 0:
                        qk_evac(1)
                    if i == 2 and not last:
                        qk_evac(0)

            with act.Fori(0, B) as b:
                qk_evac(0)
                for t in range(NT):
                    for n in range(D // T):
                        act.wait_ge(v_mm, 1)
                        act.sem_inc(v_mm, -1)
                        nc.scalar.copy(V[:, t, n * T:(n + 1) * T], bank[3 + (2 * t + n) % 3][:, :]).then_inc(v_read, 1)
                for h in range(XH):
                    s = slice(h * XKV, (h + 1) * XKV)
                    last = nc.scalar.copy(kblk[s, s], xkT[s, bass.ds(b * XKV, XKV)])
                last.then_inc(kblk_ready, 1)
                act.wait_ge(vx_mm, 1)
                act.sem_inc(vx_mm, -1)
                for h in range(XH):
                    s = slice(h * XKV, (h + 1) * XKV)
                    last = nc.scalar.copy(vblk[s, s], bank[7][s, s])
                last.then_inc(vblk_ready, 1)
                exps(0)
                with act.Fori(0, QUADS - 1) as q:
                    quad(False)
                quad(True)
                for c in range(0, PAIRS, 2):
                    from_bank(yT[:, c, :], bank[c % 4][:, :], yT_mm[0], yT_read[0])
                from_bank(hnT[:, :], bank[4][:, :], xnT_mm, xnT_evac)
                from_bank(xqT[:, :], bank[5][:, :], xq_mm, xq_read)
                act.wait_ge(xs_ready, 1)
                act.sem_inc(xs_ready, -1)
                nc.scalar.activation(xs[:, :, :], xs[:, :, :], ACT.Exp, scale=float(XHD) ** -0.5).then_inc(xs_exp, 1)
                from_bank(xpT[:, :], bank[1][:, :], xp_mm, xp_read)
                from_bank(xcT[:, :], bank[2][:, :], xc_mm, xc_read)
                from_bank(hnT[:, :], bank[4][:, :], xnT_mm, xnT_evac)
                act.wait_ge(lg_ready, 1)
                act.sem_inc(lg_ready, -1)
                nc.scalar.activation(lg[:, :, :], lg[:, :, :], ACT.Exp).then_inc(lg_exp, 1)
                from_bank(maskT[:, :], bank[6][0:E, :], mask_mm, mask_read)
                act.wait_ge(up_mm, 1)
                act.sem_inc(up_mm, -1)
                for i in range(NF):
                    nc.scalar.activation(interT[:, i, :], bank[2 + i][:, :], ACT.Gelu).then_inc(gelu_done, 1)

        @block.tensor
        def _(pe):
            mm = nc.tensor.matmul

            def transposes(n, src, dst, ready, done):
                pe.wait_ge(ready, 1)
                pe.sem_inc(ready, -1)
                for t in range(NT):
                    last = nc.tensor.transpose(dst[:, tok(t)], src(t), ident[:, :])
                last.then_inc(done, 1)

            pe.wait_ge(const_pe, 1)
            pe.sem_inc(const_pe, -1)
            pe.wait_ge(loads, 16 * len(LOADS))
            pe.wait_ge(wide_ready, 1)
            pe.sem_inc(wide_ready, -1)
            for i in range(5):
                last = mm(bank[i][:, 0:C], ones[0:1, :], rows[:, i, :], start=True, stop=(i != 0))
                if i == 0:
                    for c in range(PAIRS):
                        last = mm(bank[0][:, 0:C], bv_wide[:, c, :], w_proj[:, c, :], start=False, stop=(c == PAIRS - 1))
            last.then_inc(wide_mm, 1)
            mm(bank[5][:, 0:B * XKV], xwk[:, :], ctxT[:, :, :].rearrange("p b k -> p (b k)"), start=True, stop=True)\
                .then_inc(xk_mm, 1)
            pe.wait_ge(xk_ready, 1)
            pe.sem_inc(xk_ready, -1)

            with pe.Fori(0, B) as b:
                transposes(NT, lambda t: xn[:, t, :], bank[7], xn_ready, xnT_mm)
                pe.wait_ge(xnT_evac, 1)
                pe.sem_inc(xnT_evac, -1)
                mm(bank[6][0:HD, :], w_in[:, 0:HD], xnT[:, :], start=True, stop=True)
                mm(bank[5][0:HD, :], w_in[:, D:D + HD], xnT[:, :], start=True, stop=True).then_inc(h0_mm, 1)
                pe.wait_ge(h0_ready, 1)
                pe.sem_inc(h0_ready, -1)
                pe.sem_inc(xnT_keep, 1)
                for t in range(NT):
                    last = mm(SCORE[t], q0T[:, tok(t)], k0T[:, 0:W[t]], start=True, stop=True)
                last.then_inc(s0_mm, 1)
                pe.wait_ge(s0_ready, 1)
                pe.sem_inc(s0_ready, -1)
                dst = [bank[3][:, 0:P], bank[3][:, P:3 * P], bank[4][:, 0:W[2]], bank[5][:, :]]
                for t in range(NT):
                    last = mm(dst[t], before[:, :], tile(S0, t), start=True, stop=(t == 0))
                    for s in range(t):
                        last = mm(dst[t][:, 0:W[s]], ones[:, :], tile(S0, s), start=False, stop=(s == t - 1))
                last.then_inc(ff_mm, 1)

            def project(i, part):
                mm(bank[7][:, :], wblk[i][:, part, :], xnT[:, :], start=True, stop=True).then_inc(qk_mm, 1)

            def scores(i, half):
                s = slice(half * HD, (half + 1) * HD)
                for t in range(NT):
                    ins = mm(SCORE[t], qT[i][s, tok(t)], kT[i][s, 0:W[t]], start=True, stop=True)
                    if t:
                        ins.then_inc(score_mm, 1)

            def values(head):
                for t in range(NT):
                    for k in range(t + 1):
                        last = mm(bank[6][:, t * HD:(t + 1) * HD], probT_tile(k, t),
                                  V[:, k, bass.ds(head * HD, HD)], start=(k == 0), stop=(k == t))
                last.then_inc(pv_mm, 1)

            def turn(i, head, last, last_quad):
                s = i % 2
                for t in range(NT):
                    pe.wait_ge(exp_done, 1)
                    pe.sem_inc(exp_done, -1)
                    for k in range(t + 1):
                        at = KOFF[k] + (t - k) * P
                        ins = nc.tensor.transpose(bank[3 + at // T][:, at % T:at % T + P],
                                                  prob[s][:, QOFF[t] + k * P:QOFF[t] + (k + 1) * P], ident[:, :])
                        if t == NT - 1 and k != 1:
                            ins.then_inc(tr_mm, 1)
                if not last:
                    if i % 2:
                        pe.wait_ge(qk_ready, 1)
                        pe.sem_inc(qk_ready, -1)
                    scores((i + 1) % QUAD // 2, (i + 1) % 2)
                nxt = {0: 1, 2: 0}.get(i)
                if i == 0 or (i == 2 and not last_quad):
                    pe.wait_ge(w_ready, 1)
                    pe.sem_inc(w_ready, -1)
                    project(nxt, 0)
                pe.wait_ge(o_free, 1)
                pe.sem_inc(o_free, -1)
                pe.wait_ge(tr_read, 3)
                pe.sem_inc(tr_read, -3)
                values(head)
                if i == 0 or (i == 2 and not last_quad):
                    pe.wait_ge(qk_ready, 1)
                    pe.sem_inc(qk_ready, -1)
                    project(nxt, 1)

            with pe.Fori(0, B) as b:
                pe.wait_ge(xT_ready, 1)
                pe.sem_inc(xT_ready, -1)
                pe.wait_ge(w_ready, 1)
                pe.sem_inc(w_ready, -1)
                project(0, 0)
                pe.wait_ge(qk_ready, 1)
                pe.sem_inc(qk_ready, -1)
                project(0, 1)
                pe.wait_ge(qk_ready, 1)
                pe.sem_inc(qk_ready, -1)
                scores(0, 0)
                for t in range(NT):
                    for n in range(D // T):
                        j = 2 * t + n
                        if j >= 3:
                            pe.wait_ge(v_read, 1)
                            pe.sem_inc(v_read, -1)
                        mm(bank[3 + j % 3][:, :], xnT[:, tok(t)], w_in[:, 2 * D + n * T:2 * D + (n + 1) * T],
                           start=True, stop=True).then_inc(v_mm, 1)
                pe.wait_ge(v_read, 3)
                pe.sem_inc(v_read, -3)
                pe.wait_ge(vx_ready, 1)
                pe.sem_inc(vx_ready, -1)
                mm(bank[7][:, 0:C], ctx4[:, :, :].rearrange("p h k -> p (h k)"), xwv[:, :], start=True, stop=True)\
                    .then_inc(vx_mm, 1)
                pe.wait_ge(vblk_ready, 1)
                pe.sem_inc(vblk_ready, -1)
                with pe.Fori(0, QUADS - 1) as q:
                    for i in range(QUAD):
                        turn(i, q * QUAD + i, False, False)
                for i in range(QUAD):
                    turn(i, (QUADS - 1) * QUAD + i, i == QUAD - 1, True)

                pe.wait_ge(o_free, 1)
                for c in range(PAIRS):
                    if c >= 4:
                        pe.wait_ge(yT_read[c % 2], 1)
                        pe.sem_inc(yT_read[c % 2], -1)
                    for t in range(NT):
                        last = nc.tensor.transpose(bank[c % 4][:, tok(t)], y[:, t, c * P:(c + 1) * P], ident[:, :])
                    last.then_inc(yT_mm[c % 2], 1)
                pe.wait_ge(yT_read[0], 2)
                pe.sem_inc(yT_read[0], -2)
                pe.wait_ge(yT_read[1], 2)
                pe.sem_inc(yT_read[1], -2)
                for t in range(NT):
                    for c in range(PAIRS):
                        last = mm(bank[6][:, tok(t)], yT[:, c, tok(t)], w_proj[:, c, :], start=(c == 0),
                                  stop=(c == PAIRS - 1))
                last.then_inc(proj_mm, 1)

                transposes(NT, lambda t: xn[:, t, :], bank[4], xn_ready, xnT_mm)
                pe.wait_ge(xnT_evac, 1)
                pe.sem_inc(xnT_evac, -1)
                mm(bank[5][:, :], xwq[:, :], hnT[:, :], start=True, stop=True).then_inc(xq_mm, 1)
                pe.wait_ge(xq_read, 1)
                pe.sem_inc(xq_read, -1)
                pe.wait_ge(kblk_ready, 1)
                pe.sem_inc(kblk_ready, -1)
                for t in range(NT):
                    last = mm(bank[0][:, tok(t)], xqT[:, tok(t)], kblk[:, :], start=True, stop=True)
                last.then_inc(xs_mm, 1)
                xs_flat = xs[:, :, :].rearrange("p g k -> p (g k)")
                transposes(NT, lambda t: xs_flat[:, tok(t)], bank[1], xp_ready, xp_mm)
                pe.wait_ge(xp_read, 1)
                pe.sem_inc(xp_read, -1)
                mm(bank[2][:, :], vblk[:, :], xpT[:, :], start=True, stop=True).then_inc(xc_mm, 1)
                pe.wait_ge(xc_read, 1)
                pe.sem_inc(xc_read, -1)
                for t in range(NT):
                    last = mm(bank[3][:, tok(t)], xcT[:, tok(t)], xwo[:, :], start=True, stop=True)
                last.then_inc(xo_mm, 1)

                transposes(NT, lambda t: xn[:, t, :], bank[4], xn_ready, xnT_mm)
                pe.wait_ge(xnT_evac, 1)
                pe.sem_inc(xnT_evac, -1)
                for t in range(NT):
                    last = mm(bank[5][:, t * E:(t + 1) * E], hnT[:, tok(t)], w_r[:, :], start=True, stop=True)
                last.then_inc(lg_mm, 1)
                pe.wait_ge(pick_ready, 1)
                pe.sem_inc(pick_ready, -1)
                for t in range(NT):
                    last = mm(bank[6][0:E, tok(t)], pick[:, t, :], ident[:, :], start=True, stop=True)
                last.then_inc(mask_mm, 1)
                pe.wait_ge(mask_read, 1)
                pe.sem_inc(mask_read, -1)
                for e in range(2):
                    mm(bank[e][:, :], sel[:, e, :], maskT[:, :], start=True, stop=True).then_inc(bc_mm, 1)
                for e in range(E):
                    pe.wait_ge(xm_ready, 1)
                    pe.sem_inc(xm_ready, -1)
                    if e + 2 < E:
                        mm(bank[e % 2][:, :], sel[:, e + 2, :], maskT[:, :], start=True, stop=True).then_inc(bc_mm, 1)
                    for i in range(NF):
                        mm(bank[2 + i][:, :], w1[:, e, tok(i)], xm[:, e, :], start=(e == 0), stop=False)
                for i in range(NF):
                    last = mm(bank[2 + i][:, :], b1[:, tok(i)], maskT[:, :], start=False, stop=True)
                last.then_inc(up_mm, 1)
                pe.wait_ge(gelu_done, NF)
                pe.sem_inc(gelu_done, -NF)
                for t in range(NT):
                    for i in range(NF):
                        last = mm(bank[6][:, tok(t)], interT[:, i, tok(t)], w2[:, i, :], start=(i == 0),
                                  stop=(i == NF - 1))
                last.then_inc(down_mm, 1)

        @block.vector
        def _(dve):
            v = nc.vector

            def own(ins):
                ins.then_inc(dve_own, 1)
                dve.wait_ge(dve_own, 1)
                dve.sem_inc(dve_own, -1)

            def normalise(src):
                for t in range(NT):
                    last = v.bn_stats(stats[:, t, :], src(t))
                own(last)
                for t in range(NT):
                    last = v.bn_aggr(mv[:, t, :], stats[:, t, :])
                last.then_inc(var_ready, 1)
                dve.wait_ge(rstd_ready, 1)
                dve.sem_inc(rstd_ready, -1)
                for t in range(NT):
                    last = v.tensor_scalar(xn[:, t, :], src(t), mv[:, t, 0:1], rstd[:, t:t + 1], ALU.subtract, ALU.mult)
                return last

            dve.wait_ge(const_dve, 1)
            dve.sem_inc(const_dve, -1)
            dve.wait_ge(loads, 16 * len(LOADS))
            for c in range(PAIRS):
                last = v.tensor_scalar(bv_wide[:, c, :], ones[:, :], b_in[:, 2 * PAIRS + c:2 * PAIRS + c + 1], None,
                                       ALU.mult)
            last.then_inc(wide_ready, 1)
            dve.sem_inc(o_free, 1)

            with dve.Fori(0, B) as b:
                normalise(lambda t: x[:, bass.ds(b * NT + t, 1), :].rearrange("p o c -> p (o c)"))\
                    .then_inc(xn_ready, 1)

            def prune_round():
                for t in range(NT):
                    row = work[:, WOFF[t]:WOFF[t] + PADS + W[t]]
                    v.max(best[:, t, :], row).then_inc(pick_own[t], 1)
                for t in range(NT):
                    row = work[:, WOFF[t]:WOFF[t] + PADS + W[t]]
                    dve.wait_ge(pick_own[t], 1)
                    dve.sem_inc(pick_own[t], -1)
                    v.match_replace(row, best[:, t, :], row, MARK).then_inc(pick_own[t], 1)

            def prune_wait():
                for t in range(NT):
                    dve.wait_ge(pick_own[t], 1)
                    dve.sem_inc(pick_own[t], -1)

            def biased(s):
                for t in range(NT):
                    if t != 1:
                        dve.wait_ge(score_mm, 1)
                        dve.sem_inc(score_mm, -1)
                    v.tensor_tensor_reduce(out=tile(neg[s], t), in0=SCORE[t], in1=tile(bias, t), scale=1.0,
                                           scalar=3.0e38, op0=ALU.add, op1=ALU.min,
                                           accum_out=low[s][:, t:t + 1]).then_inc(neg_ready, 1)

            def heads_out(s, head):
                dve.wait_ge(pv_mm, 1)
                dve.sem_inc(pv_mm, -1)
                own(v.reciprocal(inv[s][:, :], total[s][:, :]))
                dve.sem_inc(head_done, 1)
                v.tensor_tensor(y[:, :, bass.ds(head * HD, HD)],
                                bank[6][:, 0:NT * HD].rearrange("p (t d) -> p t d", t=NT),
                                inv[s][:, :].unsqueeze(2).to_broadcast([P, NT, HD]), ALU.mult).then_inc(o_free, 1)

            def turn(i, head, last, prune):
                if not last:
                    biased((i + 1) % 2)
                if prune:
                    prune_wait()
                    prune_round()
                heads_out(i % 2, head)

            dve.wait_ge(work_ready, 1)
            dve.sem_inc(work_ready, -1)
            prune_round()
            with dve.Fori(0, ROUNDS - 1) as n:
                prune_wait()
                prune_round()
            prune_wait()
            dve.sem_inc(picked, 1)

            def quad(q, last):
                for i in range(QUAD):
                    turn(i, q * QUAD + i, last and i == QUAD - 1, i != QUAD - 1)

            def wide4(i):
                return wide[:, i, :].unsqueeze(1).to_broadcast([P, NT, C])

            def tiles(buf):
                return buf[:, :].rearrange("p (t c) -> p t c", t=NT)

            with dve.Fori(0, B) as b:
                dve.wait_ge(bias_ready, 1)
                dve.sem_inc(bias_ready, -1)
                biased(0)
                dve.wait_ge(work_ready, 1)
                dve.sem_inc(work_ready, -1)
                prune_round()
                with dve.Fori(0, QUADS - 1) as q:
                    quad(q, False)
                quad(QUADS - 1, True)
                prune_wait()
                dve.sem_inc(picked, 1)

                for c in range(1, PAIRS, 2):
                    dve.wait_ge(yT_mm[1], 1)
                    dve.sem_inc(yT_mm[1], -1)
                    v.tensor_copy(yT[:, c, :], bank[c % 4][:, :]).then_inc(yT_read[1], 1)
                dve.wait_ge(proj_mm, 1)
                dve.sem_inc(proj_mm, -1)
                own(v.tensor_tensor(r[:, :, :], tiles(bank[6]), x[:, bass.ds(b * NT, NT), :], ALU.add))
                own(v.tensor_tensor(r[:, :, :], r[:, :, :], wide4(0), ALU.add))
                normalise(lambda t: r[:, t, :]).then_inc(xn_ready, 1)
                dve.wait_ge(xs_mm, 1)
                dve.sem_inc(xs_mm, -1)
                xs_bank = bank[0][:, :].rearrange("p (g k) -> p g k", k=XKV)
                own(v.tensor_reduce(xmax[:, :], xs_bank, AX.X, ALU.max))
                v.tensor_tensor(xs[:, :, :], xs_bank, xmax[:, :].unsqueeze(2).to_broadcast([P, NT * XH, XKV]),
                                ALU.subtract).then_inc(xs_ready, 1)
                dve.wait_ge(xs_exp, 1)
                dve.sem_inc(xs_exp, -1)
                own(v.tensor_reduce(xsum[:, :], xs[:, :, :], AX.X, ALU.add))
                own(v.reciprocal(xsum[:, :], xsum[:, :]))
                v.tensor_tensor(xs[:, :, :], xs[:, :, :], xsum[:, :].unsqueeze(2).to_broadcast([P, NT * XH, XKV]),
                                ALU.mult).then_inc(xp_ready, 1)
                dve.wait_ge(xo_mm, 1)
                dve.sem_inc(xo_mm, -1)
                own(v.tensor_tensor(r[:, :, :], r[:, :, :], tiles(bank[3]), ALU.add))
                own(v.tensor_tensor(r[:, :, :], r[:, :, :], wide4(1), ALU.add))
                normalise(lambda t: r[:, t, :]).then_inc(xn_ready, 1)

                def each(buf):
                    return buf[:, :].unsqueeze(2).to_broadcast([P, NT, E])

                dve.wait_ge(lg_mm, 1)
                dve.sem_inc(lg_mm, -1)
                lg_bank = bank[5][:, 0:NT * E].rearrange("p (t e) -> p t e", t=NT)
                own(v.tensor_reduce(lmax[:, :], lg_bank, AX.X, ALU.max))
                v.tensor_tensor(lg[:, :, :], lg_bank, each(lmax), ALU.subtract).then_inc(lg_ready, 1)
                dve.wait_ge(lg_exp, 1)
                dve.sem_inc(lg_exp, -1)
                own(v.tensor_reduce(lsum[:, :], lg[:, :, :], AX.X, ALU.add))
                own(v.reciprocal(lsum[:, :], lsum[:, :]))
                own(v.tensor_tensor(lg[:, :, :], lg[:, :, :], each(lsum), ALU.mult))
                own(v.tensor_reduce(lmax[:, :], lg[:, :, :], AX.X, ALU.max))
                own(v.tensor_tensor(pick[:, :, :], lg[:, :, :], each(lmax), ALU.is_equal))
                own(v.tensor_tensor(pick[:, :, :], pick[:, :, :], rank[:, :, :], ALU.mult))
                own(v.tensor_reduce(lmax[:, :], pick[:, :, :], AX.X, ALU.max))
                v.tensor_tensor(pick[:, :, :], pick[:, :, :], each(lmax), ALU.is_equal).then_inc(pick_ready, 1)
                for e in range(E):
                    dve.wait_ge(bc_mm, 1)
                    dve.sem_inc(bc_mm, -1)
                    v.tensor_tensor(xm[:, e, :], bank[e % 2][:, :], hnT[:, :], ALU.mult).then_inc(xm_ready, 1)

                dve.wait_ge(res_free, 1)
                dve.sem_inc(res_free, -1)
                dve.wait_ge(down_mm, 1)
                dve.sem_inc(down_mm, -1)
                own(v.tensor_tensor(res[:, :, :], tiles(bank[6]), xn[:, :, :], ALU.add))
                own(v.tensor_tensor(res[:, :, :], res[:, :, :], wide4(2), ALU.add))
                own(normalise(lambda t: res[:, t, :]))
                own(v.tensor_tensor(xn[:, :, :], xn[:, :, :], wide4(3), ALU.mult))
                own(v.tensor_tensor(xn[:, :, :], xn[:, :, :], wide4(4), ALU.add))
                v.tensor_tensor(res[:, :, :], xn[:, :, :], r[:, :, :], ALU.add).then_inc(res_ready, 1)


_SHAPES = {"x": (P, B * NT, C), "w_in": (C, 3 * D), "b_in": (P, 3 * PAIRS), "w_proj": (P, PAIRS, C), "xwq": (C, C),
           "xwk": (CD, C), "xwv": (CD, C), "xwo": (C, C), "ctxT": (CD, B, XKV), "w_r": (C, E), "w1": (C, E, FF),
           "b1": (E, FF), "w2": (P, NF, C), "rows": (1, 5, C)}


def kernel(**inputs):
    import numpy as np
    import concourse.bacc as bacc
    from concourse.bass_utils import run_bass_kernel_spmd

    i = {k: np.asarray(v) for k, v in inputs.items()}
    laid = {
        "x": i["x"].reshape(B * NT, P, C).transpose(1, 0, 2),
        "w_in": i["L0_attn_W_attn"].T,
        "b_in": i["L0_attn_b_attn"].reshape(3 * PAIRS, P).T,
        "w_proj": i["L0_attn_W_proj"].T.reshape(PAIRS, P, C).transpose(1, 0, 2),
        "xwq": i["L0_xattn_Wq"].T,
        "xwk": i["L0_xattn_Wk"].T,
        "xwv": i["L0_xattn_Wv"].T,
        "xwo": i["L0_xattn_Wo"].T,
        "ctxT": i["ctx_768"].transpose(2, 0, 1),
        "w_r": i["L0_ffn_Wr"].T,
        "w1": i["L0_ffn_W1"].transpose(1, 0, 2),
        "b1": i["L0_ffn_b1"],
        "w2": i["L0_ffn_Wo"].reshape(NF, P, C).transpose(1, 0, 2),
        "rows": np.stack([i["L0_attn_b_proj"], i["L0_xattn_bo"], i["L0_ffn_bo"], i["L0_ffn_gamma"],
                          i["L0_ffn_beta"]])[None],
    }
    nc = bacc.Bacc("TRN2", target_bir_lowering=False, num_devices=1)
    handles = {n: nc.dram_tensor(f"in_{n}", s, F32, kind="ExternalInput").ap() for n, s in _SHAPES.items()}
    out = nc.dram_tensor("out_0", (B, T, C), F32, kind="ExternalOutput").ap()
    program(nc, handles, out)
    launched = run_bass_kernel_spmd(
        nc, [{f"in_{n}": np.ascontiguousarray(laid[n]) for n in _SHAPES}], core_ids=[0])
    return launched.results[0]["out_0"]
```

```python
from contextlib import ExitStack

import concourse.bass as bass
from concourse import mybir

F32 = mybir.dt.float32
BF16 = mybir.dt.bfloat16
ALU = mybir.AluOpType
ACT = mybir.ActivationFunctionType
AX = mybir.AxisListType

P = 128
B, T, C = 4, 512, 128
NT = T // P
H, HD = 16, 64
D = H * HD
PAIRS = H // 2
QUAD = 4
QUADS = H // QUAD
XH, XKV, CD = 4, 32, 96
XHD = C // XH
E, FF = 8, 512
NF = FF // P
W = [(t + 1) * P for t in range(NT)]
QOFF = [sum(W[:t]) for t in range(NT)]
CAUSAL = sum(W)
KOFF = [0, T, 2 * T, 2 * T - P]
BUDGET = max(1, int(T * 0.2))
KEPT = BUDGET - 1
ROUNDS = -(-KEPT // 8)
PADS = ROUNDS * 8 - KEPT
WOFF = [QOFF[t] + PADS * t for t in range(NT)]
BIG = 1.0e30
PAD = 2.0e30
MARK = -3.0e38
LN_EPS, FFN_EPS = 1e-5, 1e-12
ROUTER, RESULT = B, B + 1


def program(nc, a, out):
    with ExitStack() as ctx:
        def sb(name, shape, dt=F32):
            return ctx.enter_context(nc.sbuf_tensor(name, shape, dt))

        def sem(name):
            return ctx.enter_context(nc.semaphore(name))

        bank = [ctx.enter_context(nc.psum_tensor(f"bank{i}", [P, 512], F32)) for i in range(8)]

        ident = sb("ident", [P, P])
        ones = sb("ones", [P, P])
        before = sb("before", [P, P])
        drop = sb("drop", [P, P])
        halfpow = sb("halfpow", [P, NT])
        sel = sb("sel", [E, E, P])
        sel16 = sb("sel16", [E, E, P], BF16)
        rank = sb("rank", [P, NT, E])
        w_in = sb("w_in", [P, 3 * D])
        b_in = sb("b_in", [P, 3 * PAIRS])
        bq_neg = sb("bq_neg", [P, PAIRS])
        w_proj = sb("w_proj", [P, PAIRS, C])
        xwq = sb("xwq", [C, C])
        xwk = sb("xwk", [CD, C])
        xwv = sb("xwv", [CD, C])
        xwo = sb("xwo", [C, C])
        ctxT = sb("ctxT", [CD, B, XKV])
        ctx4 = sb("ctx4", [CD, B, XH, XKV])
        w_r = sb("w_r", [C, E])
        w1 = sb("w1", [C, E, FF])
        b1 = sb("b1", [E, FF])
        w2 = sb("w2", [P, NF, C])
        rows = sb("rows", [1, 5, C])
        wide = sb("wide", [P, 5, C])

        x = sb("x", [P, B * NT, C])
        xnT_all = sb("xnT_all", [C, B * T])
        xnT = sb("xnT", [C, T])
        stats = sb("stats", [P, (B + 2) * NT, 6])
        mv = sb("mv", [P, B + 2, NT, 2])
        rstd = sb("rstd", [P, B + 2, NT])
        q0T = [sb(f"q0T{i}", [HD, T]) for i in range(2)]
        k0T = [sb(f"k0T{i}", [HD, T]) for i in range(2)]
        F_all = sb("F_all", [P, B * CAUSAL])
        work = sb("work", [P, CAUSAL + PADS * NT])
        best = sb("best", [P, NT, 8])
        bias = sb("bias", [P, CAUSAL])
        wblk = [sb(f"wblk{i}", [C, 2, P]) for i in range(2)]
        bblk = [sb(f"bblk{i}", [P, 2]) for i in range(2)]
        qT = [sb(f"qT{i}", [P, T]) for i in range(2)]
        kT = [sb(f"kT{i}", [P, T]) for i in range(2)]
        V = sb("V", [P, NT, D])
        neg = [sb(f"neg{i}", [P, CAUSAL]) for i in range(2)]
        low = [sb(f"low{i}", [P, NT]) for i in range(2)]
        prob = [sb(f"prob{i}", [P, CAUSAL]) for i in range(2)]
        total = [sb(f"total{i}", [P, NT]) for i in range(2)]
        inv = [sb(f"inv{i}", [P, NT]) for i in range(2)]
        probT = sb("probT", [P, 3 * T])
        y = sb("y", [P, NT, D])
        y_flat = y[:, :, :].rearrange("p t d -> p (t d)")
        xn0 = y_flat[:, 0:B * NT * C].rearrange("p (t c) -> p t c", c=C)
        bv_wide = y_flat[:, B * NT * C:B * NT * C + PAIRS * P].rearrange("p (c q) -> p c q", c=PAIRS)
        interT = y_flat[:, 0:NF * T].rearrange("p (i q) -> p i q", i=NF)
        share = sb("share", [P, PAIRS * T])
        yT = share[:, :].rearrange("p (c q) -> p c q", c=PAIRS)
        xm = share[:, :].rearrange("p (e q) -> p e q", e=E)
        S0 = neg
        xn = xnT_all[:, :].rearrange("p (t c) -> p t c", c=C)
        xs_flat = w_in[:, 2 * D:2 * D + T]
        xs = xs_flat.rearrange("p (g k) -> p g k", k=XKV)
        hnT = w_in[:, 2 * D + T:2 * D + 2 * T]
        hn = F_all[:, 0:T].rearrange("p (t c) -> p t c", c=C)
        lnT = F_all[:, T:T + B * T]
        xcT = F_all[:, T + B * T:2 * T + B * T]
        maskT = F_all[0:E, 2 * T + B * T:3 * T + B * T]
        xqT, xpT = work[:, 0:T], work[:, T:2 * T]
        maskT16 = sb("maskT16", [E, T], BF16)
        kblk = sb("kblk", [P, B, P])
        vblk_all = sb("vblk_all", [P, B, P])
        vblk = sb("vblk", [P, P])
        xkT = sb("xkT", [C, B * XKV])
        mark = sb("mark", [P, 1])
        xmax = sb("xmax", [P, NT * XH])
        xsum = sb("xsum", [P, NT * XH])
        lg = sb("lg", [P, NT, E])
        lmax = sb("lmax", [P, NT])
        lsum = sb("lsum", [P, NT])
        pick = sb("pick", [P, NT, E])
        res = sb("res", [P, NT, C])

        load_x0 = sem("load_x0")
        load_x = sem("load_x")
        load_w = sem("load_w")
        load_rest = sem("load_rest")
        stored = sem("stored")
        pool_own = sem("pool_own")
        dve_own = sem("dve_own")
        const_pe = sem("const_pe")
        const_dve = sem("const_dve")
        act_own = sem("act_own")
        wide_ready = sem("wide_ready")
        wide_mm = sem("wide_mm")
        wide_done = sem("wide_done")
        xk_mm = sem("xk_mm")
        x_biased = sem("x_biased")
        var_ready = sem("var_ready")
        rstd_ready = sem("rstd_ready")
        xn_ready = sem("xn_ready")
        hn_ready = sem("hn_ready")
        res_norm = sem("res_norm")
        xn_copied = sem("xn_copied")
        x_plus = sem("x_plus")
        xnT_mm = sem("xnT_mm")
        xnT_read = sem("xnT_read")
        h0_mm = sem("h0_mm")
        h0_ready = sem("h0_ready")
        s0_mm = sem("s0_mm")
        s0_relu = sem("s0_relu")
        s0_ready = sem("s0_ready")
        ff_mm = sem("ff_mm")
        ff_read = sem("ff_read")
        ff_ready = sem("ff_ready")
        ctx4_ready = sem("ctx4_ready")
        vx_mm = sem("vx_mm")
        vx_read = sem("vx_read")
        vblk_ready = sem("vblk_ready")
        work_ready = sem("work_ready")
        work_free = sem("work_free")
        picked = sem("picked")
        xT_ready = sem("xT_ready")
        w_ready = sem("w_ready")
        v_mm = sem("v_mm")
        v_read = sem("v_read")
        qk_mm = sem("qk_mm")
        qk_ready = sem("qk_ready")
        score_mm = sem("score_mm")
        neg_ready = sem("neg_ready")
        exp_done = sem("exp_done")
        tr_mm = sem("tr_mm")
        tr_read = sem("tr_read")
        pv_mm = sem("pv_mm")
        o_free = sem("o_free")
        head_done = sem("head_done")
        yT_mm_act = sem("yT_mm_act")
        yT_mm_dve = sem("yT_mm_dve")
        yT_read_act = sem("yT_read_act")
        yT_read_dve = sem("yT_read_dve")
        proj_mm = sem("proj_mm")
        xq_mm = sem("xq_mm")
        xq_read = sem("xq_read")
        xs_mm = sem("xs_mm")
        xs_ready = sem("xs_ready")
        xs_exp = sem("xs_exp")
        xp_ready = sem("xp_ready")
        xp_mm = sem("xp_mm")
        xp_read = sem("xp_read")
        xc_mm = sem("xc_mm")
        xc_read = sem("xc_read")
        xo_mm = sem("xo_mm")
        ln_mm = sem("ln_mm")
        ln_read = sem("ln_read")
        lg_mm = sem("lg_mm")
        lg_ready = sem("lg_ready")
        lg_exp = sem("lg_exp")
        pick_ready = sem("pick_ready")
        mask_mm = sem("mask_mm")
        mask_read = sem("mask_read")
        bc_mm = sem("bc_mm")
        xm_ready = sem("xm_ready")
        up_mm = sem("up_mm")
        gelu_done = sem("gelu_done")
        down_mm = sem("down_mm")
        res_ready = sem("res_ready")
        res_free = sem("res_free")
        pick_own = [sem(f"pick_own{t}") for t in range(NT)]

        def tok(t):
            return slice(t * P, (t + 1) * P)

        def tile(buf, t):
            return buf[:, QOFF[t]:QOFF[t] + W[t]]

        def work_row(t):
            return work[:, WOFF[t] + PADS:WOFF[t] + PADS + W[t]]

        SCORE = [bank[0][:, 0:W[0]], bank[0][:, W[0]:W[0] + W[1]], bank[1][:, 0:W[2]], bank[2][:, 0:W[3]]]
        FFOUT = [bank[3][:, 0:W[0]], bank[3][:, W[0]:W[0] + W[1]], bank[4][:, 0:W[2]], bank[5][:, 0:W[3]]]

        YBANKS, YBANKS_LAST = [7, 3, 4, 5], [0, 1, 2, 3]

        def probT_tile(k, t):
            return probT[:, KOFF[k] + (t - k) * P:KOFF[k] + (t - k + 1) * P]

        LOAD_W = [(w_in[:, :], a["w_in"]), (b_in[:, :], a["b_in"])]
        LOAD_REST = [
            (w_proj[:, :, :], a["w_proj"]), (rows[:, :, :], a["rows"]), (xwk[:, :], a["xwk"]),
            (xwv[:, :], a["xwv"]), (ctxT[:, :, :], a["ctxT"]), (xwq[:, :], a["xwq"]), (xwo[:, :], a["xwo"]),
            (w_r[:, :], a["w_r"]), (b1[:, :], a["b1"]), (w2[:, :, :], a["w2"]), (w1[:, :, :], a["w1"]),
        ]
        REST = 16 * len(LOAD_REST)

        block = ctx.enter_context(nc.Block())

        @block.sync
        def _(sp):
            for b in range(B):
                sp.dma_start(x[:, b * NT:(b + 1) * NT, :], a["x"][:, b * NT:(b + 1) * NT, :])\
                    .then_inc(load_x if b else load_x0, 16)
                if b == 0:
                    for dst, src in LOAD_W:
                        sp.dma_start(dst, src).then_inc(load_w, 16)
            for dst, src in LOAD_REST:
                sp.dma_start(dst, src).then_inc(load_rest, 16)
            sp.sem_inc(res_free, 1)
            with sp.Fori(0, B) as b:
                sp.wait_ge(res_ready, 1)
                sp.sem_inc(res_ready, -1)
                sp.dma_start(out[bass.ds(b, 1), :, :].rearrange("o (t p) c -> p (o t) c", p=P),
                             res[:, :, :]).then_inc(stored, 16)
                sp.wait_ge(stored, 16)
                sp.sem_inc(stored, -16)
                sp.sem_inc(res_free, 1)

        @block.gpsimd
        def _(pool):
            def own(ins):
                ins.then_inc(pool_own, 1)
                pool.wait_ge(pool_own, 1)
                pool.sem_inc(pool_own, -1)

            def power(b, eps):
                pool.wait_ge(var_ready, 1)
                pool.sem_inc(var_ready, -1)
                own(nc.gpsimd.tensor_scalar(rstd[:, b, :], mv[:, b, :, 1], eps, None, ALU.add))
                nc.gpsimd.tensor_tensor(rstd[:, b, :], rstd[:, b, :], halfpow[:, :], ALU.pow).then_inc(rstd_ready, 1)

            def head0_mask(b):
                pool.wait_ge(s0_relu, 1)
                pool.sem_inc(s0_relu, -1)
                for t in range(NT):
                    last = nc.gpsimd.affine_select(out=S0[b % 2][:, QOFF[t] + t * P:QOFF[t] + W[t]],
                                                   in_=S0[b % 2][:, QOFF[t] + t * P:QOFF[t] + W[t]],
                                                   compare_op=ALU.is_gt, fill=0.0, base=0, pattern=[[-1, P]],
                                                   channel_multiplier=1)
                own(last)
                for t in range(NT):
                    last = nc.gpsimd.memset(S0[b % 2][:, QOFF[t]:QOFF[t] + 1], 0.0)
                last.then_inc(s0_ready, 1)

            def ff_mask(b):
                pool.wait_ge(ff_read, 1)
                pool.sem_inc(ff_read, -1)
                for t in range(NT):
                    d = F_all[:, b * CAUSAL + QOFF[t] + t * P:b * CAUSAL + QOFF[t] + W[t]]
                    last = nc.gpsimd.affine_select(out=d, in_=d, compare_op=ALU.is_ge, fill=-BIG, base=0,
                                                   pattern=[[-1, P]], channel_multiplier=1)
                own(last)

            def fill_work(b):
                for t in range(NT):
                    nc.gpsimd.memset(work[:, WOFF[t]:WOFF[t] + PADS], PAD)
                    last = nc.gpsimd.tensor_copy(work_row(t), F_all[:, bass.ds(b * CAUSAL + QOFF[t], W[t])])
                last.then_inc(work_ready, 1)

            def fill_weights(i, pair):
                nc.gpsimd.tensor_copy(wblk[i][:, 0, :], w_in[:, bass.ds(pair * P, P)])
                nc.gpsimd.tensor_copy(bblk[i][:, 0:1], bq_neg[:, bass.ds(pair, 1)])
                nc.gpsimd.tensor_copy(bblk[i][:, 1:2], b_in[:, bass.ds(pair + PAIRS, 1)])
                nc.gpsimd.tensor_copy(wblk[i][:, 1, :], w_in[:, bass.ds(pair * P + D, P)]).then_inc(w_ready, 1)

            def batch_inputs(b):
                nc.gpsimd.tensor_copy(xnT[:, :], xnT_all[:, bass.ds(b * T, T)]).then_inc(xT_ready, 1)
                for i in range(2):
                    fill_weights(i, i)

            nc.gpsimd.memset(halfpow[:, :], -0.5)
            own(nc.gpsimd.memset(ones[:, :], 1.0))
            own(nc.gpsimd.affine_select(out=ident[:, :], in_=ones[:, :], compare_op=ALU.is_equal, fill=0.0, base=0,
                                        pattern=[[-1, P]], channel_multiplier=1))
            own(nc.gpsimd.affine_select(out=before[:, :], in_=ones[:, :], compare_op=ALU.is_gt, fill=0.0, base=0,
                                        pattern=[[1, P]], channel_multiplier=-1))
            pool.sem_inc(const_pe, 1)
            power(0, LN_EPS)
            for b in range(1, B):
                power(b, LN_EPS)
            own(nc.gpsimd.memset(drop[:, :], BIG))
            nc.gpsimd.affine_select(out=drop[:, :], in_=drop[:, :], compare_op=ALU.not_equal, fill=0.0, base=0,
                                    pattern=[[-1, P]], channel_multiplier=1)
            for e in range(E):
                last = nc.gpsimd.memset(rank[:, :, e:e + 1], float(E - e))
            own(last)
            pool.sem_inc(const_dve, 1)
            head0_mask(0)
            ff_mask(0)
            fill_work(0)
            for b in range(1, B):
                head0_mask(b)
                ff_mask(b)
            own(nc.gpsimd.memset(sel[:, :, :], 1.0))
            own(nc.gpsimd.affine_select(out=sel[:, :, :], in_=sel[:, :, :], compare_op=ALU.is_equal, fill=0.0,
                                        base=0, pattern=[[-1, E], [0, P]], channel_multiplier=1))
            own(nc.gpsimd.tensor_copy(sel16[:, :, :], sel[:, :, :]))
            batch_inputs(0)
            pool.wait_ge(wide_done, 1)
            pool.sem_inc(wide_done, -1)
            for b in range(B):
                last = nc.gpsimd.tensor_tensor(x[:, b * NT:(b + 1) * NT, :], x[:, b * NT:(b + 1) * NT, :],
                                               wide[:, 0, :].unsqueeze(1).to_broadcast([P, NT, C]), ALU.add)
            last.then_inc(x_biased, 1)

            def quads_inputs():
                with pool.Fori(0, QUADS - 1) as q:
                    pool.wait_ge(head_done, 1)
                    pool.sem_inc(head_done, -1)
                    fill_weights(0, q * 2 + 2)
                    pool.wait_ge(head_done, 2)
                    pool.sem_inc(head_done, -2)
                    fill_weights(1, q * 2 + 3)
                    pool.wait_ge(head_done, 1)
                    pool.sem_inc(head_done, -1)

            with pool.Fori(0, B - 1) as b:
                pool.wait_ge(work_free, 1)
                pool.sem_inc(work_free, -1)
                fill_work(b + 1)
                quads_inputs()
                pool.wait_ge(head_done, 2)
                pool.sem_inc(head_done, -2)
                batch_inputs(b + 1)
                pool.wait_ge(head_done, QUAD - 2)
                pool.sem_inc(head_done, -(QUAD - 2))
            for b in range(B - 1):
                power(b, LN_EPS)
            quads_inputs()

            def add_bias(b):
                nc.gpsimd.tensor_tensor(x[:, b * NT:(b + 1) * NT, :], x[:, b * NT:(b + 1) * NT, :],
                                        wide[:, 1, :].unsqueeze(1).to_broadcast([P, NT, C]), ALU.add)\
                    .then_inc(x_plus, 1)

            def vblk_copy(b):
                nc.gpsimd.tensor_copy(vblk[:, :], vblk_all[:, bass.ds(b, 1), :].rearrange("p o c -> p (o c)"))\
                    .then_inc(vblk_ready, 1)

            def result(b):
                power(RESULT, FFN_EPS)
                pool.wait_ge(res_norm, 1)
                pool.sem_inc(res_norm, -1)
                for row, op in ((3, ALU.mult), (4, ALU.add)):
                    own(nc.gpsimd.tensor_tensor(res[:, :, :], res[:, :, :],
                                                wide[:, row, :].unsqueeze(1).to_broadcast([P, NT, C]), op))
                nc.gpsimd.tensor_tensor(res[:, :, :], res[:, :, :], x[:, bass.ds(b * NT, NT), :], ALU.add)\
                    .then_inc(res_ready, 1)

            vblk_copy(0)
            pool.wait_ge(xn_copied, 1)
            pool.sem_inc(xn_copied, -1)
            for b in range(B - 1):
                add_bias(b)
            power(ROUTER, LN_EPS)
            power(B - 1, LN_EPS)
            pool.wait_ge(xn_copied, 1)
            pool.sem_inc(xn_copied, -1)
            add_bias(B - 1)
            with pool.Fori(0, B - 1) as b:
                vblk_copy(b + 1)
                power(ROUTER, LN_EPS)
                result(b)
            result(B - 1)

        @block.scalar
        def _(act):
            copy, activation = nc.scalar.copy, nc.scalar.activation

            def from_bank(dst, src, got, read):
                act.wait_ge(got, 1)
                act.sem_inc(got, -1)
                copy(dst, src).then_inc(read, 1)

            def turned(b):
                from_bank(xnT_all[:, b * T:(b + 1) * T], bank[7][:, :], xnT_mm, xnT_read)

            def head0(b):
                act.wait_ge(h0_mm, 1)
                act.sem_inc(h0_mm, -1)
                activation(q0T[b % 2][:, :], bank[6][0:HD, :], ACT.Identity, scale=-0.125, bias=bq_neg[0:HD, 0:1])
                act.wait_ge(h0_mm, 1)
                act.sem_inc(h0_mm, -1)
                activation(k0T[b % 2][:, :], bank[7][0:HD, :], ACT.Identity, bias=b_in[0:HD, PAIRS:PAIRS + 1])\
                    .then_inc(h0_ready, 1)

            def relu(b):
                act.wait_ge(s0_mm, 1)
                act.sem_inc(s0_mm, -1)
                for t in range(NT):
                    last = activation(tile(S0[b % 2], t), SCORE[t], ACT.Relu, scale=-1.0)
                last.then_inc(s0_relu, 1)

            def ff_out(b):
                act.wait_ge(ff_mm, 1)
                act.sem_inc(ff_mm, -1)
                for t in range(NT):
                    last = activation(F_all[:, b * CAUSAL + QOFF[t]:b * CAUSAL + QOFF[t] + W[t]], FFOUT[t], ACT.Copy,
                                      scale=-1.0)
                last.then_inc(ff_read, 1)

            act.wait_ge(load_w, 16 * len(LOAD_W))
            activation(bq_neg[:, :], b_in[:, 0:PAIRS], ACT.Copy, scale=-0.125).then_inc(act_own, 1)
            act.wait_ge(act_own, 1)
            act.sem_inc(act_own, -1)
            turned(0)
            head0(0)
            turned(1)
            relu(0)
            head0(1)
            ff_out(0)
            turned(2)
            relu(1)
            head0(2)
            ff_out(1)
            turned(3)
            relu(2)
            head0(3)
            ff_out(2)
            relu(3)
            ff_out(3)
            nc.scalar.activation(kblk[:, :, :], F_all[:, 0:B * P].rearrange("p (b c) -> p b c", b=B), ACT.Copy,
                                 scale=0.0)
            nc.scalar.activation(vblk_all[:, :, :], F_all[:, 0:B * P].rearrange("p (b c) -> p b c", b=B), ACT.Copy,
                                 scale=0.0).then_inc(act_own, 1)
            act.wait_ge(act_own, 1)
            act.sem_inc(act_own, -1)
            act.sem_inc(ff_ready, 1)
            act.wait_ge(wide_mm, 1)
            act.sem_inc(wide_mm, -1)
            for i in range(5):
                last = copy(wide[:, i, :], bank[i][:, 0:C])
            last.then_inc(wide_done, 1)
            act.wait_ge(xk_mm, 1)
            act.sem_inc(xk_mm, -1)
            copy(xkT[:, :], bank[5][:, 0:B * XKV]).then_inc(act_own, 1)
            act.wait_ge(act_own, 1)
            act.sem_inc(act_own, -1)
            for h in range(XH):
                s = slice(h * XKV, (h + 1) * XKV)
                copy(kblk[s, :, s], xkT[s, :].rearrange("p (b k) -> p b k", b=B))
            act.wait_ge(vx_mm, 1)
            act.sem_inc(vx_mm, -1)
            for h in range(XH):
                s = slice(h * XKV, (h + 1) * XKV)
                last = copy(vblk_all[s, :, s], bank[6][s, :].rearrange("p (b k) -> p b k", b=B)[:, :, s])
            last.then_inc(vx_read, 1)

            def qk_evac(i):
                act.wait_ge(qk_mm, 1)
                act.sem_inc(qk_mm, -1)
                activation(qT[i][:, :], bank[7][:, :], ACT.Identity, scale=-0.125, bias=bblk[i][:, 0:1])\
                    .then_inc(qk_ready, 1)
                act.wait_ge(qk_mm, 1)
                act.sem_inc(qk_mm, -1)
                activation(kT[i][:, :], bank[7][:, :], ACT.Identity, bias=bblk[i][:, 1:2]).then_inc(qk_ready, 1)

            def exps(s):
                for t in range(NT):
                    act.wait_ge(neg_ready, 1)
                    act.sem_inc(neg_ready, -1)
                    activation(tile(prob[s], t), tile(neg[s], t), ACT.Exp, scale=-1.0, bias=low[s][:, t:t + 1],
                               accum_out=total[s][:, t:t + 1]).then_inc(exp_done, 1)

            def probT_evac():
                for i, n in ((0, T), (2, T // 2), (1, T)):
                    act.wait_ge(tr_mm, 1)
                    act.sem_inc(tr_mm, -1)
                    copy(probT[:, i * T:i * T + n], bank[3 + i][:, 0:n]).then_inc(tr_read, 1)

            def quad(last):
                for i in range(QUAD):
                    probT_evac()
                    if not (last and i == QUAD - 1):
                        exps((i + 1) % 2)
                    if i == 0:
                        qk_evac(1)
                    if i == 2 and not last:
                        qk_evac(0)

            def batch_start():
                qk_evac(0)
                for t in range(NT):
                    for n in range(D // T):
                        act.wait_ge(v_mm, 1)
                        act.sem_inc(v_mm, -1)
                        copy(V[:, t, n * T:(n + 1) * T], bank[3 + (2 * t + n) % 3][:, :]).then_inc(v_read, 1)
                exps(0)

            def projection(banks):
                for c in range(0, PAIRS, 2):
                    act.wait_ge(yT_mm_act, 1)
                    act.sem_inc(yT_mm_act, -1)
                    copy(yT[:, c, :], bank[banks[c % 4]][:, :]).then_inc(yT_read_act, 1)

            batch_start()
            with act.Fori(0, B - 1) as b:
                with act.Fori(0, QUADS - 1) as q:
                    quad(False)
                quad(True)
                batch_start()
                projection(YBANKS)

            def ln_evac(bank_, dst):
                from_bank(dst, bank[bank_][:, :], ln_mm, ln_read)

            def q_evac(bank_):
                from_bank(xqT, bank[bank_][:, :], xq_mm, xq_read)

            def xs_exps():
                act.wait_ge(xs_ready, 1)
                act.sem_inc(xs_ready, -1)
                activation(xs, xs, ACT.Exp, scale=float(XHD) ** -0.5).then_inc(xs_exp, 1)

            def probs_evac(bank_):
                from_bank(xpT, bank[bank_][:, :], xp_mm, xp_read)

            def context_evac(bank_):
                from_bank(xcT, bank[bank_][:, :], xc_mm, xc_read)

            def logit_exps():
                act.wait_ge(lg_ready, 1)
                act.sem_inc(lg_ready, -1)
                activation(lg[:, :, :], lg[:, :, :], ACT.Exp).then_inc(lg_exp, 1)

            def mask_evac(bank_):
                act.wait_ge(mask_mm, 1)
                act.sem_inc(mask_mm, -1)
                copy(maskT16[:, :], bank[bank_][0:E, :])
                copy(maskT, bank[bank_][0:E, :]).then_inc(mask_read, 1)

            with act.Fori(0, QUADS - 1) as q:
                quad(False)
            probT_evac()
            exps(1)
            qk_evac(1)
            probT_evac()
            exps(0)
            ln_evac(7, lnT[:, 0:T])
            q_evac(7)
            probT_evac()
            exps(1)
            xs_exps()
            probT_evac()
            probs_evac(7)
            context_evac(7)
            projection(YBANKS_LAST)
            ln_evac(4, lnT[:, T:2 * T])
            ln_evac(5, lnT[:, 2 * T:3 * T])
            ln_evac(7, hnT)
            logit_exps()
            mask_evac(7)

            def gelus():
                for i in range(NF):
                    act.wait_ge(up_mm, 1)
                    act.sem_inc(up_mm, -1)
                    activation(interT[:, i, :], bank[2 + i][:, :], ACT.Gelu).then_inc(gelu_done, 1)

            ln_evac(6, lnT[:, (B - 1) * T:B * T])
            with act.Fori(0, B - 1) as b:
                q_evac(6)
                xs_exps()
                probs_evac(6)
                context_evac(6)
                ln_evac(6, hnT)
                logit_exps()
                gelus()
                mask_evac(6)
            gelus()

        @block.tensor
        def _(pe):
            mm = nc.tensor.matmul

            def transposes(src, dst, ready, done):
                pe.wait_ge(ready, 1)
                pe.sem_inc(ready, -1)
                for t in range(NT):
                    last = nc.tensor.transpose(dst[:, tok(t)], src(t), ident[:, :])
                last.then_inc(done, 1)

            def turned(b):
                transposes(lambda t: xn0[:, b * NT + t, :], bank[7], xn_ready, xnT_mm)

            def head0(b):
                pe.wait_ge(xnT_read, 1)
                pe.sem_inc(xnT_read, -1)
                mm(bank[6][0:HD, :], w_in[:, 0:HD], xnT_all[:, b * T:(b + 1) * T], start=True, stop=True)\
                    .then_inc(h0_mm, 1)
                mm(bank[7][0:HD, :], w_in[:, D:D + HD], xnT_all[:, b * T:(b + 1) * T], start=True, stop=True)\
                    .then_inc(h0_mm, 1)

            def head0_scores(b):
                for t in range(NT):
                    last = mm(SCORE[t], q0T[b % 2][:, tok(t)], k0T[b % 2][:, 0:W[t]], start=True, stop=True)
                last.then_inc(s0_mm, 1)

            def ff(b):
                pe.wait_ge(s0_ready, 1)
                pe.sem_inc(s0_ready, -1)
                for t in range(NT):
                    last = mm(FFOUT[t], before[:, :], tile(S0[b % 2], t), start=True, stop=(t == 0))
                    for s in range(t):
                        last = mm(FFOUT[t][:, 0:W[s]], ones[:, :], tile(S0[b % 2], s), start=False, stop=(s == t - 1))
                last.then_inc(ff_mm, 1)

            pe.wait_ge(const_pe, 1)
            pe.sem_inc(const_pe, -1)
            pe.wait_ge(load_w, 16 * len(LOAD_W))
            turned(0)
            head0(0)
            for b in range(B):
                pe.wait_ge(h0_ready, 1)
                pe.sem_inc(h0_ready, -1)
                if b + 1 < B:
                    turned(b + 1)
                head0_scores(b)
                if b + 1 < B:
                    head0(b + 1)
                ff(b)

            pe.wait_ge(load_rest, REST)
            pe.wait_ge(wide_ready, 1)
            pe.sem_inc(wide_ready, -1)
            mm(bank[0][:, 0:C], ones[0:1, :], rows[:, 0, :], start=True, stop=False)
            for c in range(PAIRS):
                mm(bank[0][:, 0:C], bv_wide[:, c, :], w_proj[:, c, :], start=False, stop=(c == PAIRS - 1))
            for i in range(1, 5):
                if i == 3:
                    pe.wait_ge(ff_ready, 1)
                    pe.sem_inc(ff_ready, -1)
                last = mm(bank[i][:, 0:C], ones[0:1, :], rows[:, i, :], start=True, stop=True)
            last.then_inc(wide_mm, 1)
            mm(bank[5][:, 0:B * XKV], xwk[:, :], ctxT[:, :, :].rearrange("p b k -> p (b k)"), start=True, stop=True)\
                .then_inc(xk_mm, 1)
            pe.wait_ge(ctx4_ready, 1)
            pe.sem_inc(ctx4_ready, -1)
            for b in range(B):
                last = mm(bank[6][:, tok(b)], ctx4[:, b, :, :].rearrange("p h k -> p (h k)"), xwv[:, :],
                          start=True, stop=True)
            last.then_inc(vx_mm, 1)
            pe.wait_ge(vx_read, 1)
            pe.sem_inc(vx_read, -1)

            def project(i, part):
                mm(bank[7][:, :], wblk[i][:, part, :], xnT[:, :], start=True, stop=True).then_inc(qk_mm, 1)

            def scores(i, half):
                s = slice(half * HD, (half + 1) * HD)
                for t in range(NT):
                    ins = mm(SCORE[t], qT[i][s, tok(t)], kT[i][s, 0:W[t]], start=True, stop=True)
                    if t:
                        ins.then_inc(score_mm, 1)

            def values(head):
                for t in range(NT):
                    for k in range(t + 1):
                        last = mm(bank[6][:, t * HD:(t + 1) * HD], probT_tile(k, t),
                                  V[:, k, bass.ds(head * HD, HD)], start=(k == 0), stop=(k == t))
                last.then_inc(pv_mm, 1)

            def transpose_probs(s):
                for t in range(NT):
                    pe.wait_ge(exp_done, 1)
                    pe.sem_inc(exp_done, -1)
                    for k in range(t + 1):
                        at = KOFF[k] + (t - k) * P
                        ins = nc.tensor.transpose(bank[3 + at // T][:, at % T:at % T + P],
                                                  prob[s][:, QOFF[t] + k * P:QOFF[t] + (k + 1) * P], ident[:, :])
                        if t == NT - 1 and k != 1:
                            ins.then_inc(tr_mm, 1)

            def turn(i, head, more):
                transpose_probs(i % 2)
                if i % 2:
                    pe.wait_ge(qk_ready, 1)
                    pe.sem_inc(qk_ready, -1)
                scores((i + 1) % QUAD // 2, (i + 1) % 2)
                if more:
                    pe.wait_ge(w_ready, 1)
                    pe.sem_inc(w_ready, -1)
                    project((i // 2 + 1) % 2, 0)
                pe.wait_ge(o_free, 1)
                pe.sem_inc(o_free, -1)
                pe.wait_ge(tr_read, 3)
                pe.sem_inc(tr_read, -3)
                values(head)
                if more:
                    pe.wait_ge(qk_ready, 1)
                    pe.sem_inc(qk_ready, -1)
                    project((i // 2 + 1) % 2, 1)

            def batch_start():
                pe.wait_ge(xT_ready, 1)
                pe.sem_inc(xT_ready, -1)
                pe.wait_ge(w_ready, 1)
                pe.sem_inc(w_ready, -1)
                project(0, 0)
                pe.wait_ge(qk_ready, 1)
                pe.sem_inc(qk_ready, -1)
                project(0, 1)
                for t in range(NT):
                    for n in range(D // T):
                        j = 2 * t + n
                        if j >= 3:
                            pe.wait_ge(v_read, 1)
                            pe.sem_inc(v_read, -1)
                        mm(bank[3 + j % 3][:, :], xnT[:, tok(t)], w_in[:, 2 * D + n * T:2 * D + (n + 1) * T],
                           start=True, stop=True).then_inc(v_mm, 1)
                        if j == 3:
                            pe.wait_ge(qk_ready, 1)
                            pe.sem_inc(qk_ready, -1)
                            scores(0, 0)
                pe.wait_ge(v_read, 3)
                pe.sem_inc(v_read, -3)

            LAST_QUAD = (QUADS - 1) * QUAD

            def last_turn(i, head):
                transpose_probs(i % 2)
                pe.wait_ge(o_free, 1)
                pe.sem_inc(o_free, -1)
                pe.wait_ge(tr_read, 3)
                pe.sem_inc(tr_read, -3)
                values(head)

            def yT_bank(c, banks):
                if c >= 4 and c % 2 == 0:
                    pe.wait_ge(yT_read_act, 1)
                    pe.sem_inc(yT_read_act, -1)
                if c >= 4 and c % 2 == 1:
                    pe.wait_ge(yT_read_dve, 1)
                    pe.sem_inc(yT_read_dve, -1)
                for t in range(NT):
                    last = nc.tensor.transpose(bank[banks[c % 4]][:, tok(t)], y[:, t, c * P:(c + 1) * P], ident[:, :])
                last.then_inc(yT_mm_dve if c % 2 else yT_mm_act, 1)

            def project_tile(t):
                for c in range(PAIRS):
                    last = mm(bank[6][:, tok(t)], yT[:, c, tok(t)], w_proj[:, c, :], start=(c == 0),
                              stop=(c == PAIRS - 1))
                if t == NT - 1:
                    last.then_inc(proj_mm, 1)

            batch_start()
            with pe.Fori(0, B - 1) as b:
                with pe.Fori(0, QUADS - 1) as q:
                    for i in range(QUAD):
                        turn(i, q * QUAD + i, i % 2 == 0)
                for i in range(QUAD - 1):
                    turn(i, LAST_QUAD + i, i == 0)
                last_turn(QUAD - 1, H - 1)
                batch_start()
                pe.wait_ge(o_free, 1)
                pe.sem_inc(o_free, -1)
                for c in range(PAIRS):
                    yT_bank(c, YBANKS)
                pe.wait_ge(yT_read_act, 2)
                pe.sem_inc(yT_read_act, -2)
                pe.wait_ge(yT_read_dve, 2)
                pe.sem_inc(yT_read_dve, -2)
                for t in range(NT):
                    project_tile(t)

            def ln1(b, to):
                transposes(lambda t: xn[:, b * NT + t, :], to, xn_ready, ln_mm)

            def xq(b, to):
                mm(to[:, :], xwq[:, :], lnT[:, bass.ds(b * T, T)], start=True, stop=True).then_inc(xq_mm, 1)

            def xscore(b, to):
                pe.wait_ge(xq_read, 1)
                pe.sem_inc(xq_read, -1)
                for t in range(NT):
                    last = mm(to[:, tok(t)], xqT[:, tok(t)],
                              kblk[:, bass.ds(b, 1), :].rearrange("p o c -> p (o c)"), start=True, stop=True)
                last.then_inc(xs_mm, 1)

            def xprobs(b, to):
                transposes(lambda t: xs_flat[:, tok(t)], to, xp_ready, xp_mm)

            def context(b, to):
                pe.wait_ge(xp_read, 1)
                pe.sem_inc(xp_read, -1)
                pe.wait_ge(vblk_ready, 1)
                pe.sem_inc(vblk_ready, -1)
                mm(to[:, :], vblk[:, :], xpT, start=True, stop=True).then_inc(xc_mm, 1)

            def xout(b, to):
                pe.wait_ge(xc_read, 1)
                pe.sem_inc(xc_read, -1)
                for t in range(NT):
                    last = mm(to[:, tok(t)], xcT[:, tok(t)], xwo[:, :], start=True, stop=True)
                last.then_inc(xo_mm, 1)

            def ln2(b, to):
                transposes(lambda t: hn[:, t, :], to, hn_ready, ln_mm)

            def logits(b, to):
                pe.wait_ge(ln_read, 1)
                pe.sem_inc(ln_read, -1)
                for t in range(NT):
                    last = mm(to[:, t * E:(t + 1) * E], hnT[:, tok(t)], w_r[:, :], start=True, stop=True)
                last.then_inc(lg_mm, 1)

            def mask(b, to):
                pe.wait_ge(pick_ready, 1)
                pe.sem_inc(pick_ready, -1)
                for t in range(NT):
                    last = mm(to[0:E, tok(t)], pick[:, t, :], ident[:, :], start=True, stop=True)
                last.then_inc(mask_mm, 1)

            side = bank[7]
            with pe.Fori(0, QUADS - 1) as q:
                for i in range(QUAD):
                    turn(i, q * QUAD + i, i % 2 == 0)
            turn(0, LAST_QUAD, True)
            transpose_probs(1)
            pe.wait_ge(qk_ready, 1)
            pe.sem_inc(qk_ready, -1)
            scores(1, 0)
            ln1(0, side)
            pe.wait_ge(o_free, 1)
            pe.sem_inc(o_free, -1)
            pe.wait_ge(tr_read, 3)
            pe.sem_inc(tr_read, -3)
            values(LAST_QUAD + 1)
            pe.wait_ge(ln_read, 1)
            pe.sem_inc(ln_read, -1)
            xq(0, side)
            transpose_probs(0)
            scores(1, 1)
            xscore(0, side)
            pe.wait_ge(o_free, 1)
            pe.sem_inc(o_free, -1)
            pe.wait_ge(tr_read, 3)
            pe.sem_inc(tr_read, -3)
            values(LAST_QUAD + 2)
            transpose_probs(1)
            xprobs(0, side)
            pe.wait_ge(o_free, 1)
            pe.sem_inc(o_free, -1)
            pe.wait_ge(tr_read, 3)
            pe.sem_inc(tr_read, -3)
            values(LAST_QUAD + 3)
            context(0, side)
            pe.wait_ge(o_free, 1)
            pe.sem_inc(o_free, -1)
            yT_bank(0, YBANKS_LAST)
            yT_bank(1, YBANKS_LAST)
            xout(0, side)
            for c in range(2, PAIRS):
                yT_bank(c, YBANKS_LAST)
            pe.wait_ge(yT_read_act, 2)
            pe.sem_inc(yT_read_act, -2)
            pe.wait_ge(yT_read_dve, 2)
            pe.sem_inc(yT_read_dve, -2)
            ln1(1, bank[4])
            ln1(2, bank[5])
            project_tile(0)
            pe.wait_ge(ln_read, 2)
            pe.sem_inc(ln_read, -2)
            ln2(0, side)
            project_tile(1)
            logits(0, side)
            project_tile(2)
            project_tile(3)
            mask(0, side)
            pe.wait_ge(o_free, 1)
            pe.sem_inc(o_free, -1)

            def spread_mask(e):
                mm(bank[e % 2][:, :], sel16[:, e, :], maskT16[:, :], start=True, stop=True).then_inc(bc_mm, 1)

            def experts_start():
                pe.wait_ge(mask_read, 1)
                pe.sem_inc(mask_read, -1)
                spread_mask(0)
                spread_mask(1)
                for i in range(NF):
                    mm(bank[2 + i][:, :], b1[:, tok(i)], maskT, start=True, stop=False)

            MASK_AT = {0: 2, 1: 3, 4: 4, 5: 5, 8: 6, 9: 7}
            STEP_AT = {0: xq, 2: xscore, 9: xprobs, 11: context, 13: xout, 21: ln2, 23: logits}

            def experts(steps, b):
                for n in range(E * NF):
                    e, i = divmod(n, NF)
                    if n in MASK_AT:
                        pe.wait_ge(xm_ready, 1)
                        pe.sem_inc(xm_ready, -1)
                        spread_mask(MASK_AT[n])
                    if i == 0 and e >= E - 2:
                        pe.wait_ge(xm_ready, 1)
                        pe.sem_inc(xm_ready, -1)
                    ins = mm(bank[2 + i][:, :], w1[:, e, tok(i)], xm[:, e, :], start=False, stop=(e == E - 1))
                    if e == E - 1:
                        ins.then_inc(up_mm, 1)
                    if n in steps:
                        steps[n](b, bank[6])

            def down():
                pe.wait_ge(gelu_done, NF)
                pe.sem_inc(gelu_done, -NF)
                for t in range(NT):
                    for i in range(NF):
                        last = mm(bank[7][:, tok(t)], interT[:, i, tok(t)], w2[:, i, :], start=(i == 0),
                                  stop=(i == NF - 1))
                last.then_inc(down_mm, 1)

            experts_start()
            ln1(B - 1, bank[6])
            pe.wait_ge(ln_read, 1)
            pe.sem_inc(ln_read, -1)
            with pe.Fori(0, B - 1) as b:
                experts(STEP_AT, b + 1)
                mask(b + 1, bank[6])
                down()
                experts_start()
            experts({}, None)
            down()

        @block.vector
        def _(dve):
            v = nc.vector

            def own(ins):
                ins.then_inc(dve_own, 1)
                dve.wait_ge(dve_own, 1)
                dve.sem_inc(dve_own, -1)

            def moments(src, slot):
                for t in range(NT):
                    last = v.bn_stats(stats[:, slot * NT + t, :], src(t))
                own(last)
                for t in range(NT):
                    last = v.bn_aggr(mv[:, slot, t, :], stats[:, slot * NT + t, :])
                last.then_inc(var_ready, 1)

            def normalise(src, slot, dst):
                dve.wait_ge(rstd_ready, 1)
                dve.sem_inc(rstd_ready, -1)
                for t in range(NT):
                    last = v.tensor_scalar(dst(t), src(t), mv[:, slot, t, 0:1], rstd[:, slot, t:t + 1], ALU.subtract,
                                           ALU.mult)
                return last

            for b in range(B):
                if b == 0:
                    dve.wait_ge(load_x0, 16)
                if b == 1:
                    dve.wait_ge(load_x, 16 * (B - 1))
                moments(lambda t: x[:, b * NT + t, :], b)
                if b == 0:
                    normalise(lambda t: x[:, t, :], 0, lambda t: xn0[:, t, :]).then_inc(xn_ready, 1)
            for b in range(1, B):
                normalise(lambda t: x[:, b * NT + t, :], b, lambda t: xn0[:, b * NT + t, :]).then_inc(xn_ready, 1)
            dve.wait_ge(const_dve, 1)
            dve.sem_inc(const_dve, -1)
            dve.wait_ge(load_w, 16 * len(LOAD_W))
            for c in range(PAIRS):
                last = v.tensor_scalar(bv_wide[:, c, :], ones[:, :], b_in[:, 2 * PAIRS + c:2 * PAIRS + c + 1], None,
                                       ALU.mult)
            last.then_inc(wide_ready, 1)
            dve.wait_ge(load_rest, REST)
            for h in range(XH):
                last = v.tensor_copy(ctx4[:, :, h, :], ctxT[:, :, :])
            last.then_inc(ctx4_ready, 1)
            dve.sem_inc(o_free, 1)

            def prune_round():
                for t in range(NT):
                    row = work[:, WOFF[t]:WOFF[t] + PADS + W[t]]
                    v.max(best[:, t, :], row).then_inc(pick_own[t], 1)
                for t in range(NT):
                    row = work[:, WOFF[t]:WOFF[t] + PADS + W[t]]
                    dve.wait_ge(pick_own[t], 1)
                    dve.sem_inc(pick_own[t], -1)
                    v.match_replace(row, best[:, t, :], row, MARK).then_inc(pick_own[t], 1)

            def prune_wait():
                for t in range(NT):
                    dve.wait_ge(pick_own[t], 1)
                    dve.sem_inc(pick_own[t], -1)

            def make_bias(b):
                for t in range(NT):
                    if t:
                        v.tensor_scalar(bias[:, QOFF[t]:QOFF[t] + t * P], work_row(t)[:, 0:t * P], -PAD, BIG, ALU.is_gt,
                                        ALU.mult)
                    last = v.scalar_tensor_tensor(out=bias[:, QOFF[t] + t * P:QOFF[t] + W[t]],
                                                  in0=work_row(t)[:, t * P:W[t]], scalar=-PAD, in1=drop[:, :],
                                                  op0=ALU.is_gt, op1=ALU.mult)
                own(last)
                dve.sem_inc(work_free, 1)
                last = v.tensor_tensor(bias[:, :], bias[:, :], F_all[:, bass.ds(b * CAUSAL, CAUSAL)], ALU.subtract)
                own(last)

            def biased(s):
                for t in range(NT):
                    if t != 1:
                        dve.wait_ge(score_mm, 1)
                        dve.sem_inc(score_mm, -1)
                    v.tensor_tensor_reduce(out=tile(neg[s], t), in0=SCORE[t], in1=tile(bias, t), scale=1.0,
                                           scalar=3.0e38, op0=ALU.add, op1=ALU.min,
                                           accum_out=low[s][:, t:t + 1]).then_inc(neg_ready, 1)

            def head_out(s, head):
                dve.wait_ge(pv_mm, 1)
                dve.sem_inc(pv_mm, -1)
                own(v.reciprocal(inv[s][:, :], total[s][:, :]))
                dve.sem_inc(head_done, 1)
                v.tensor_tensor(y[:, :, bass.ds(head * HD, HD)],
                                bank[6][:, 0:NT * HD].rearrange("p (t d) -> p t d", t=NT),
                                inv[s][:, :].unsqueeze(2).to_broadcast([P, NT, HD]), ALU.mult).then_inc(o_free, 1)

            def yT_evac(c, banks):
                dve.wait_ge(yT_mm_dve, 1)
                dve.sem_inc(yT_mm_dve, -1)
                v.tensor_copy(yT[:, c, :], bank[banks[c % 4]][:, :]).then_inc(yT_read_dve, 1)

            def projection_add(b):
                dve.wait_ge(proj_mm, 1)
                dve.sem_inc(proj_mm, -1)
                rows_b = x[:, bass.ds(b * NT, NT), :]
                return v.tensor_tensor(rows_b, bank[6][:, :].rearrange("p (t c) -> p t c", t=NT), rows_b, ALU.add)

            dve.wait_ge(work_ready, 1)
            dve.sem_inc(work_ready, -1)
            prune_round()
            with dve.Fori(0, ROUNDS - 1) as n:
                prune_wait()
                prune_round()
            prune_wait()
            make_bias(0)
            dve.wait_ge(x_biased, 1)
            dve.sem_inc(x_biased, -1)
            biased(0)

            with dve.Fori(0, B - 1) as b:
                dve.wait_ge(work_ready, 1)
                dve.sem_inc(work_ready, -1)
                prune_round()
                with dve.Fori(0, QUADS - 1) as q:
                    for i in range(QUAD):
                        biased((i + 1) % 2)
                        prune_wait()
                        prune_round()
                        head_out(i % 2, q * QUAD + i)
                for i in range(QUAD):
                    if i < QUAD - 1:
                        biased((i + 1) % 2)
                    head_out(i % 2, (QUADS - 1) * QUAD + i)
                    if i == QUAD - 2:
                        prune_wait()
                        make_bias(b + 1)
                biased(0)
                for c in range(1, PAIRS, 2):
                    yT_evac(c, YBANKS)
                projection_add(b).then_inc(o_free, 1)
            def wide4(i):
                return wide[:, i, :].unsqueeze(1).to_broadcast([P, NT, C])

            def tiles(buf):
                return buf[:, :].rearrange("p (t c) -> p t c", t=NT)

            def rows_of(b):
                return x[:, bass.ds(b * NT, NT), :]

            def row_of(b):
                return lambda t: x[:, bass.ds(b * NT + t, 1), :].rearrange("p o c -> p (o c)")

            def attend_norm(b):
                normalise(row_of(b), b, lambda t: xn[:, b * NT + t, :]).then_inc(xn_ready, 1)

            def copied():
                v.memset(mark[:, :], 0.0).then_inc(xn_copied, 1)

            def xs_minus_max(side):
                dve.wait_ge(xs_mm, 1)
                dve.sem_inc(xs_mm, -1)
                xs_bank = side[:, :].rearrange("p (g k) -> p g k", k=XKV)
                own(v.tensor_reduce(xmax[:, :], xs_bank, AX.X, ALU.max))
                v.tensor_tensor(xs, xs_bank, xmax[:, :].unsqueeze(2).to_broadcast([P, NT * XH, XKV]),
                                ALU.subtract).then_inc(xs_ready, 1)

            def xs_divide():
                dve.wait_ge(xs_exp, 1)
                dve.sem_inc(xs_exp, -1)
                own(v.tensor_reduce(xsum[:, :], xs, AX.X, ALU.add))
                own(v.reciprocal(xsum[:, :], xsum[:, :]))
                v.tensor_tensor(xs, xs, xsum[:, :].unsqueeze(2).to_broadcast([P, NT * XH, XKV]),
                                ALU.mult).then_inc(xp_ready, 1)

            def attend_add(b, side):
                dve.wait_ge(xo_mm, 1)
                dve.sem_inc(xo_mm, -1)
                dve.wait_ge(x_plus, 1)
                dve.sem_inc(x_plus, -1)
                own(v.tensor_tensor(rows_of(b), tiles(side), rows_of(b), ALU.add))
                moments(row_of(b), ROUTER)

            def route_norm(b):
                normalise(row_of(b), ROUTER, lambda t: hn[:, t, :]).then_inc(hn_ready, 1)

            def each(buf):
                return buf[:, :].unsqueeze(2).to_broadcast([P, NT, E])

            def route(side):
                dve.wait_ge(lg_mm, 1)
                dve.sem_inc(lg_mm, -1)
                lg_bank = side[:, 0:NT * E].rearrange("p (t e) -> p t e", t=NT)
                own(v.tensor_reduce(lmax[:, :], lg_bank, AX.X, ALU.max))
                v.tensor_tensor(lg[:, :, :], lg_bank, each(lmax), ALU.subtract).then_inc(lg_ready, 1)
                dve.wait_ge(lg_exp, 1)
                dve.sem_inc(lg_exp, -1)
                own(v.tensor_reduce(lsum[:, :], lg[:, :, :], AX.X, ALU.add))
                own(v.reciprocal(lsum[:, :], lsum[:, :]))
                own(v.tensor_tensor(lg[:, :, :], lg[:, :, :], each(lsum), ALU.mult))
                own(v.tensor_reduce(lmax[:, :], lg[:, :, :], AX.X, ALU.max))
                own(v.tensor_tensor(pick[:, :, :], lg[:, :, :], each(lmax), ALU.is_equal))
                own(v.tensor_tensor(pick[:, :, :], pick[:, :, :], rank[:, :, :], ALU.mult))
                own(v.tensor_reduce(lmax[:, :], pick[:, :, :], AX.X, ALU.max))
                v.tensor_tensor(pick[:, :, :], pick[:, :, :], each(lmax), ALU.is_equal).then_inc(pick_ready, 1)

            def expert_inputs(lo, hi):
                for e in range(lo, hi):
                    dve.wait_ge(bc_mm, 1)
                    dve.sem_inc(bc_mm, -1)
                    v.tensor_tensor(xm[:, e, :], bank[e % 2][:, :], hnT, ALU.mult).then_inc(xm_ready, 1)

            def start_result():
                dve.wait_ge(res_free, 1)
                dve.sem_inc(res_free, -1)
                own(v.tensor_tensor(res[:, :, :], hn, wide4(2), ALU.add))

            def down_out():
                dve.wait_ge(down_mm, 1)
                dve.sem_inc(down_mm, -1)
                own(v.tensor_tensor(res[:, :, :], tiles(bank[7]), res[:, :, :], ALU.add))

            for b in range(B - 1):
                moments(row_of(b), b)
            for b in range(B - 1):
                attend_norm(b)
            copied()
            with dve.Fori(0, QUADS - 1) as q:
                for i in range(QUAD):
                    biased((i + 1) % 2)
                    head_out(i % 2, q * QUAD + i)
            biased(1)
            head_out(0, H - 4)
            biased(0)
            head_out(1, H - 3)
            biased(1)
            xs_minus_max(bank[7])
            xs_divide()
            head_out(0, H - 2)
            head_out(1, H - 1)
            yT_evac(1, YBANKS_LAST)
            yT_evac(3, YBANKS_LAST)
            attend_add(0, bank[7])
            yT_evac(5, YBANKS_LAST)
            yT_evac(7, YBANKS_LAST)
            route_norm(0)
            route(bank[7])
            own(projection_add(B - 1))
            dve.sem_inc(o_free, 1)
            moments(row_of(B - 1), B - 1)
            expert_inputs(0, 2)
            attend_norm(B - 1)
            copied()
            with dve.Fori(0, B - 1) as b:
                expert_inputs(2, 4)
                xs_minus_max(bank[6])
                expert_inputs(4, 6)
                xs_divide()
                expert_inputs(6, 8)
                attend_add(b + 1, bank[6])
                start_result()
                route_norm(b + 1)
                route(bank[6])
                down_out()
                expert_inputs(0, 2)
                moments(lambda t: res[:, t, :], RESULT)
                normalise(lambda t: res[:, t, :], RESULT, lambda t: res[:, t, :]).then_inc(res_norm, 1)
            expert_inputs(2, E)
            start_result()
            down_out()
            moments(lambda t: res[:, t, :], RESULT)
            normalise(lambda t: res[:, t, :], RESULT, lambda t: res[:, t, :]).then_inc(res_norm, 1)


_SHAPES = {"x": (P, B * NT, C), "w_in": (C, 3 * D), "b_in": (P, 3 * PAIRS), "w_proj": (P, PAIRS, C), "xwq": (C, C),
           "xwk": (CD, C), "xwv": (CD, C), "xwo": (C, C), "ctxT": (CD, B, XKV), "w_r": (C, E), "w1": (C, E, FF),
           "b1": (E, FF), "w2": (P, NF, C), "rows": (1, 5, C)}


def kernel(**inputs):
    import numpy as np
    import concourse.bacc as bacc
    from concourse.bass_utils import run_bass_kernel_spmd

    i = {k: np.asarray(v) for k, v in inputs.items()}
    laid = {
        "x": i["x"].reshape(B * NT, P, C).transpose(1, 0, 2),
        "w_in": i["L0_attn_W_attn"].T,
        "b_in": i["L0_attn_b_attn"].reshape(3 * PAIRS, P).T,
        "w_proj": i["L0_attn_W_proj"].T.reshape(PAIRS, P, C).transpose(1, 0, 2),
        "xwq": i["L0_xattn_Wq"].T,
        "xwk": i["L0_xattn_Wk"].T,
        "xwv": i["L0_xattn_Wv"].T,
        "xwo": i["L0_xattn_Wo"].T,
        "ctxT": i["ctx_768"].transpose(2, 0, 1),
        "w_r": i["L0_ffn_Wr"].T,
        "w1": i["L0_ffn_W1"].transpose(1, 0, 2),
        "b1": i["L0_ffn_b1"],
        "w2": i["L0_ffn_Wo"].reshape(NF, P, C).transpose(1, 0, 2),
        "rows": np.stack([i["L0_attn_b_proj"], i["L0_xattn_bo"], i["L0_ffn_bo"], i["L0_ffn_gamma"],
                          i["L0_ffn_beta"]])[None],
    }
    nc = bacc.Bacc("TRN2", target_bir_lowering=False, num_devices=1)
    handles = {n: nc.dram_tensor(f"in_{n}", s, F32, kind="ExternalInput").ap() for n, s in _SHAPES.items()}
    out = nc.dram_tensor("out_0", (B, T, C), F32, kind="ExternalOutput").ap()
    program(nc, handles, out)
    launched = run_bass_kernel_spmd(
        nc, [{f"in_{n}": np.ascontiguousarray(laid[n]) for n in _SHAPES}], core_ids=[0])
    return launched.results[0]["out_0"]
```

```python
from contextlib import ExitStack

import concourse.bass as bass
from concourse import mybir

F32 = mybir.dt.float32
F32R = mybir.dt.float32r
BF16 = mybir.dt.bfloat16
ALU = mybir.AluOpType
ACT = mybir.ActivationFunctionType
AX = mybir.AxisListType

P = 128
B, T, C = 4, 512, 128
NT = T // P
H, HD = 16, 64
D = H * HD
PAIRS = H // 2
QUAD = 4
QUADS = H // QUAD
XH, XKV, CD = 4, 32, 96
XHD = C // XH
E, FF = 8, 512
NF = FF // P
W = [(t + 1) * P for t in range(NT)]
QOFF = [sum(W[:t]) for t in range(NT)]
CAUSAL = sum(W)
KOFF = [0, T, 2 * T, 2 * T - P]
BUDGET = max(1, int(T * 0.2))
KEPT = BUDGET - 1
ROUNDS = -(-KEPT // 8)
PADS = ROUNDS * 8 - KEPT
WOFF = [QOFF[t] + PADS * t for t in range(NT)]
BIG = 1.0e30
PAD = 2.0e30
MARK = -3.0e38
LN_EPS, FFN_EPS = 1e-5, 1e-12
ROUTER, RESULT = B, B + 1


def program(nc, a, out):
    with ExitStack() as ctx:
        def sb(name, shape, dt=F32):
            return ctx.enter_context(nc.sbuf_tensor(name, shape, dt))

        def sem(name):
            return ctx.enter_context(nc.semaphore(name))

        bank = [ctx.enter_context(nc.psum_tensor(f"bank{i}", [P, 512], F32)) for i in range(8)]

        ident = sb("ident", [P, P])
        ones = sb("ones", [P, P])
        before = sb("before", [P, P])
        drop = sb("drop", [P, P])
        halfpow = sb("halfpow", [P, NT])
        sel16 = sb("sel16", [E, E, P], BF16)
        rank = sb("rank", [P, NT, E])
        w_in = sb("w_in", [P, 3 * D])
        b_in = sb("b_in", [P, 3 * PAIRS])
        bq_neg = sb("bq_neg", [P, PAIRS])
        w_proj = sb("w_proj", [P, PAIRS, C])
        xwq = sb("xwq", [C, C])
        xwk = sb("xwk", [CD, C])
        xwv = sb("xwv", [CD, C])
        xwo = sb("xwo", [C, C])
        ctxT = sb("ctxT", [CD, B, XKV])
        w_r = sb("w_r", [C, E])
        with nc.sbuf_tensor("w1", [C, E, FF], F32) as w1:
            pass
        w1h = sb("w1h", [C, E, FF], F32R)
        b1_part = sb("b1_part", [3 * E, FF], BF16)
        b1_parts = sb("b1_parts", [3 * E, FF], BF16)
        w2 = sb("w2", [P, NF, C])
        wide = sb("wide", [P, 5, C])

        x = sb("x", [P, B * NT, C])
        xnT_all = sb("xnT_all", [C, B * T])
        xh, xl = sb("xh", [C, T], F32R), sb("xl", [C, T], F32R)
        wvh, wvl = sb("wvh", [C, D], F32R), sb("wvl", [C, D], F32R)
        stats = sb("stats", [P, (B + 2) * NT, 6])
        mv = sb("mv", [P, B + 2, NT, 2])
        rstd = sb("rstd", [P, B + 2, NT])
        with nc.sbuf_tensor("F_all", [P, B * CAUSAL], F32) as F_all:
            pass
        late = sb("late", [P, T])
        w1l = sb("w1l", [C, E, FF], F32R)
        maskT16 = sb("maskT16", [3 * E, T], BF16)
        lg = sb("lg", [P, NT, E])
        pick = sb("pick", [P, NT, E])
        pick3 = sb("pick3", [P, NT, 3 * E])
        sb("late_pad", [P, B * CAUSAL - T - E * FF - T // 2 - 5 * NT * E])
        work = sb("work", [P, CAUSAL + PADS * NT])
        best = sb("best", [P, NT, 8])
        bias = sb("bias", [P, CAUSAL])
        wh = sb("wh", [C, 2, P], F32R)
        wl = sb("wl", [C, 2, P], F32R)
        qk = sb("qk", [P, 2, T])
        qkh = [sb(f"qkh{i}", [P, 2, T], F32R) for i in range(2)]
        qkl = [sb(f"qkl{i}", [P, 2, T], F32R) for i in range(2)]
        V = sb("V", [P, NT, D])
        neg = [sb(f"neg{i}", [P, CAUSAL]) for i in range(2)]
        low = [sb(f"low{i}", [P, NT]) for i in range(2)]
        prob = [sb(f"prob{i}", [P, CAUSAL]) for i in range(2)]
        total = [sb(f"total{i}", [P, NT]) for i in range(2)]
        inv = [sb(f"inv{i}", [P, NT]) for i in range(2)]
        probT = sb("probT", [P, 3 * T])
        y = sb("y", [P, NT, D])
        y_flat = y[:, :, :].rearrange("p t d -> p (t d)")
        xn0 = y_flat[:, 0:B * NT * C].rearrange("p (t c) -> p t c", c=C)
        bv_wide = y_flat[:, B * NT * C:B * NT * C + PAIRS * P].rearrange("p (c q) -> p c q", c=PAIRS)
        rows = y_flat[0:1, 3 * D:3 * D + 5 * C].rearrange("p (r c) -> p r c", c=C)
        interT = y_flat[:, 0:NF * T].rearrange("p (i q) -> p i q", i=NF)
        share = sb("share", [P, PAIRS * T])
        yT = share[:, :].rearrange("p (c q) -> p c q", c=PAIRS)
        V_flat = V[:, :, :].rearrange("p t d -> p (t d)")
        q0T = [V_flat[0:HD, i * T:(i + 1) * T] for i in range(2)]
        k0T = [V_flat[0:HD, (i + 2) * T:(i + 3) * T] for i in range(2)]
        ctx4 = share[0:CD, 0:T].rearrange("p (b h k) -> p b h k", b=B, h=XH)
        b1 = share[0:3 * E, 2 * T:2 * T + FF]
        b1_rest = share[0:3 * E, 3 * T:3 * T + FF]
        xkT = share[:, T:T + B * XKV]
        res = bias[:, 0:NT * C].rearrange("p (t c) -> p t c", c=C)
        S0 = neg
        xn = xnT_all[:, :].rearrange("p (t c) -> p t c", c=C)
        xs_flat = w_in[:, 2 * D:2 * D + T]
        xs = xs_flat.rearrange("p (g k) -> p g k", k=XKV)
        hnT = w_in[:, 2 * D + T:2 * D + 2 * T]
        hn = late[:, 0:T].rearrange("p (t c) -> p t c", c=C)
        lnT = w_in[:, 0:2 * D]
        xqT, xpT = work[:, 0:T], work[:, T:2 * T]
        xcT = xqT
        hnh, hnl = qkh[0][:, 0, :], qkh[0][:, 1, :]
        xm = [qkh[1], qkl[0], qkl[1]]
        w1_high = wvh[:, 0:FF]
        kblk = sb("kblk", [P, B, P])
        vblk_all = sb("vblk_all", [P, B, P])
        vblk = sb("vblk", [P, P])
        mark = sb("mark", [P, 1 + B])
        act_mark = sb("act_mark", [P, 1])
        xmax = sb("xmax", [P, NT * XH])
        xsum = sb("xsum", [P, NT * XH])
        lmax = sb("lmax", [P, NT])
        lsum = sb("lsum", [P, NT])

        load_x0 = sem("load_x0")
        load_x = sem("load_x")
        load_w = sem("load_w")
        load_rest = sem("load_rest")
        stored = sem("stored")
        pool_own = sem("pool_own")
        dve_own = sem("dve_own")
        const_pe = sem("const_pe")
        const_dve = sem("const_dve")
        act_own = sem("act_own")
        wide_ready = sem("wide_ready")
        wide_mm = sem("wide_mm")
        wide_read = sem("wide_read")
        wide_done = sem("wide_done")
        var_ready = sem("var_ready")
        rstd_ready = sem("rstd_ready")
        xn_ready = sem("xn_ready")
        hn_ready = sem("hn_ready")
        beta_added = sem("beta_added")
        xn_copied = sem("xn_copied")
        x_plus = sem("x_plus")
        xnT_mm = sem("xnT_mm")
        xnT_read = sem("xnT_read")
        h0_mm = sem("h0_mm")
        h0_ready = sem("h0_ready")
        s0_mm = sem("s0_mm")
        s0_relu = sem("s0_relu")
        s0_ready = sem("s0_ready")
        ff_mm = sem("ff_mm")
        ff_read = sem("ff_read")
        ff_ready = sem("ff_ready")
        ctx4_ready = sem("ctx4_ready")
        vx_mm = sem("vx_mm")
        vx_read = sem("vx_read")
        vblk_ready = sem("vblk_ready")
        F_ready = sem("F_ready")
        xh_ready = sem("xh_ready")
        w_ready = sem("w_ready")
        wv_high = sem("wv_high")
        wv_ready = sem("wv_ready")
        lo_in = sem("lo_in")
        inv_ready = sem("inv_ready")
        last_exps = sem("last_exps")
        v_mm = sem("v_mm")
        v_read = sem("v_read")
        qk_mm = sem("qk_mm")
        qk_ready = sem("qk_ready")
        score_mm = sem("score_mm")
        neg_ready = sem("neg_ready")
        exp_done = sem("exp_done")
        tr_mm = sem("tr_mm")
        tr_read = sem("tr_read")
        pv_mm = sem("pv_mm")
        o_free = sem("o_free")
        yT_mm_act = sem("yT_mm_act")
        yT_mm_dve = sem("yT_mm_dve")
        yT_read_act = sem("yT_read_act")
        yT_read_dve = sem("yT_read_dve")
        proj_mm = sem("proj_mm")
        xq_mm = sem("xq_mm")
        xq_read = sem("xq_read")
        xs_mm = sem("xs_mm")
        xs_ready = sem("xs_ready")
        xs_exp = sem("xs_exp")
        xp_ready = sem("xp_ready")
        xp_mm = sem("xp_mm")
        xp_read = sem("xp_read")
        xc_mm = sem("xc_mm")
        xc_read = sem("xc_read")
        xo_mm = sem("xo_mm")
        ln_mm = sem("ln_mm")
        ln_read = sem("ln_read")
        lg_mm = sem("lg_mm")
        lg_ready = sem("lg_ready")
        lg_exp = sem("lg_exp")
        pick_ready = sem("pick_ready")
        hnh_ready = sem("hnh_ready")
        hn_split = sem("hn_split")
        mask_mm = sem("mask_mm")
        mask_read = sem("mask_read")
        bc_mm = sem("bc_mm")
        xm_ready = sem("xm_ready")
        up_mm = sem("up_mm")
        gelu_done = sem("gelu_done")
        down_mm = sem("down_mm")
        res_ready = sem("res_ready")
        res_free = sem("res_free")
        pick_own = [sem(f"pick_own{t}") for t in range(NT)]

        def tok(t):
            return slice(t * P, (t + 1) * P)

        def tile(buf, t):
            return buf[:, QOFF[t]:QOFF[t] + W[t]]

        def work_row(t):
            return work[:, WOFF[t] + PADS:WOFF[t] + PADS + W[t]]

        SCORE = [bank[0][:, 0:W[0]], bank[0][:, W[0]:W[0] + W[1]], bank[1][:, 0:W[2]], bank[2][:, 0:W[3]]]
        FFOUT = [bank[3][:, 0:W[0]], bank[3][:, W[0]:W[0] + W[1]], bank[4][:, 0:W[2]], bank[5][:, 0:W[3]]]

        YBANKS, YBANKS_LAST = [6, 5, 3, 4], [0, 1, 2, 3]

        def probT_tile(k, t):
            return probT[:, KOFF[k] + (t - k) * P:KOFF[k] + (t - k + 1) * P]

        LOAD_W = [(w_in[:, :], a["w_in"]), (b_in[:, :], a["b_in"])]
        LOAD_REST = [
            (w_proj[:, :, :], a["w_proj"]), (rows[:, :, :], a["rows"]), (xwk[:, :], a["xwk"]),
            (xwv[:, :], a["xwv"]), (ctxT[:, :, :], a["ctxT"]), (xwq[:, :], a["xwq"]), (xwo[:, :], a["xwo"]),
            *((b1[i * E:(i + 1) * E, :], a["b1"]) for i in range(3)), (w_r[:, :], a["w_r"]),
            (w2[:, :, :], a["w2"]), (w1[:, :, :], a["w1"]),
        ]
        REST = 16 * len(LOAD_REST)

        block = ctx.enter_context(nc.Block())

        @block.sync
        def _(sp):
            for b in range(B):
                sp.dma_start(x[:, b * NT:(b + 1) * NT, :], a["x"][:, b * NT:(b + 1) * NT, :])\
                    .then_inc(load_x if b else load_x0, 16)
                if b == 0:
                    for dst, src in LOAD_W:
                        sp.dma_start(dst, src).then_inc(load_w, 16)
            for dst, src in LOAD_REST:
                sp.dma_start(dst, src).then_inc(load_rest, 16)
            sp.sem_inc(res_free, 1)
            with sp.Fori(0, B) as b:
                sp.wait_ge(res_ready, 1)
                sp.sem_inc(res_ready, -1)
                sp.dma_start(out[bass.ds(b, 1), :, :].rearrange("o (t p) c -> p (o t) c", p=P),
                             res[:, :, :]).then_inc(stored, 16)
                sp.wait_ge(stored, 16)
                sp.sem_inc(stored, -16)
                sp.sem_inc(res_free, 1)

        @block.gpsimd
        def _(pool):
            def own(ins):
                ins.then_inc(pool_own, 1)
                pool.wait_ge(pool_own, 1)
                pool.sem_inc(pool_own, -1)

            def power(b, eps):
                pool.wait_ge(var_ready, 1)
                pool.sem_inc(var_ready, -1)
                own(nc.gpsimd.tensor_scalar(rstd[:, b, :], mv[:, b, :, 1], eps, None, ALU.add))
                nc.gpsimd.tensor_tensor(rstd[:, b, :], rstd[:, b, :], halfpow[:, :], ALU.pow).then_inc(rstd_ready, 1)

            def head0_mask(b):
                for t in range(NT):
                    pool.wait_ge(s0_relu, 1)
                    pool.sem_inc(s0_relu, -1)
                    own(nc.gpsimd.affine_select(out=S0[b % 2][:, QOFF[t] + t * P:QOFF[t] + W[t]],
                                                in_=S0[b % 2][:, QOFF[t] + t * P:QOFF[t] + W[t]],
                                                compare_op=ALU.is_gt, fill=0.0, base=0, pattern=[[-1, P]],
                                                channel_multiplier=1))
                    nc.gpsimd.memset(S0[b % 2][:, QOFF[t]:QOFF[t] + 1], 0.0).then_inc(s0_ready, 1)

            def ff_mask(b):
                for t in range(NT):
                    pool.wait_ge(ff_read, 1)
                    pool.sem_inc(ff_read, -1)
                    d = F_all[:, b * CAUSAL + QOFF[t] + t * P:b * CAUSAL + QOFF[t] + W[t]]
                    nc.gpsimd.affine_select(out=d, in_=d, compare_op=ALU.is_ge, fill=-BIG, base=0,
                                            pattern=[[-1, P]], channel_multiplier=1).then_inc(F_ready, 1)

            def split_low(low_, full, high):
                return nc.gpsimd.tensor_tensor(low_, full, high.bitcast(F32), ALU.subtract)

            def fill_weights(pair):
                pair_w = w_in[:, 0:2 * D].rearrange("p (k d) -> p k d", k=2)[:, :, bass.ds(pair * P, P)]
                own(nc.gpsimd.tensor_copy(wh[:, :, :], pair_w))
                split_low(wl[:, :, :], pair_w, wh[:, :, :]).then_inc(w_ready, 1)

            def split_qk(i, part):
                pool.wait_ge(lo_in, 2)
                pool.sem_inc(lo_in, -2)
                split_low(qkl[i][:, part, :], qk[:, part, :], qkh[i][:, part, :]).then_inc(qk_ready, 1)

            def bias_rest(part, src):
                own(nc.gpsimd.tensor_copy(b1_part[:, :], src))
                own(nc.gpsimd.affine_select(out=b1_part[:, :], in_=b1_part[:, :], compare_op=ALU.is_ge, fill=0.0,
                                            base=-E * part, pattern=[[0, FF]], channel_multiplier=1))
                own(nc.gpsimd.tensor_tensor(b1_rest, src, b1_part[:, :], ALU.subtract))

            def batch_inputs(b):
                pool.wait_ge(xh_ready, 1)
                pool.sem_inc(xh_ready, -1)
                split_low(xl[:, :], xnT_all[:, bass.ds(b * T, T)], xh[:, :])

            nc.gpsimd.memset(halfpow[:, :], -0.5)
            own(nc.gpsimd.memset(ones[:, :], 1.0))
            own(nc.gpsimd.affine_select(out=ident[:, :], in_=ones[:, :], compare_op=ALU.is_equal, fill=0.0, base=0,
                                        pattern=[[-1, P]], channel_multiplier=1))
            own(nc.gpsimd.affine_select(out=before[:, :], in_=ones[:, :], compare_op=ALU.is_gt, fill=0.0, base=0,
                                        pattern=[[1, P]], channel_multiplier=-1))
            pool.sem_inc(const_pe, 1)
            power(0, LN_EPS)
            for b in range(1, B):
                power(b, LN_EPS)
            own(nc.gpsimd.memset(drop[:, :], BIG))
            nc.gpsimd.affine_select(out=drop[:, :], in_=drop[:, :], compare_op=ALU.not_equal, fill=0.0, base=0,
                                    pattern=[[-1, P]], channel_multiplier=1)
            for e in range(E):
                last = nc.gpsimd.memset(rank[:, :, e:e + 1], float(E - e))
            own(last)
            pool.sem_inc(const_dve, 1)
            head0_mask(0)
            ff_mask(0)
            head0_mask(1)
            pool.wait_ge(load_rest, REST)
            bias_rest(1, b1)
            ff_mask(1)
            batch_inputs(0)
            fill_weights(0)
            head0_mask(2)
            bias_rest(2, b1_rest)
            ff_mask(2)
            head0_mask(3)
            split_qk(0, 0)
            pool.wait_ge(wv_high, 1)
            pool.sem_inc(wv_high, -1)
            split_low(wvl[:, :], w_in[:, 2 * D:3 * D], wvh[:, :]).then_inc(wv_ready, 1)
            ff_mask(3)
            split_qk(0, 1)

            def quads():
                with pool.Fori(0, QUADS - 1) as q:
                    for i in range(QUAD):
                        if i % 2 == 0:
                            split_qk((i // 2 + 1) % 2, 1)
                            fill_weights(q * 2 + 2 + i // 2)
                        else:
                            split_qk((i // 2) % 2, 0)

            fill_weights(1)
            pool.wait_ge(wide_done, 1)
            pool.sem_inc(wide_done, -1)
            for b in range(B):
                nc.gpsimd.tensor_tensor(x[:, b * NT:(b + 1) * NT, :], x[:, b * NT:(b + 1) * NT, :],
                                        wide[:, 0, :].unsqueeze(1).to_broadcast([P, NT, C]), ALU.add)
            split_qk(1, 0)
            nc.gpsimd.tensor_copy(b1_parts[:, :], b1_rest)
            own(nc.gpsimd.memset(sel16[:, :, :], 1.0))
            own(nc.gpsimd.affine_select(out=sel16[:, :, :], in_=sel16[:, :, :], compare_op=ALU.is_equal, fill=0.0,
                                        base=0, pattern=[[-1, E], [0, P]], channel_multiplier=1))
            with pool.Fori(0, B - 1) as b:
                quads()
                split_qk(1, 1)
                batch_inputs(b + 1)
                fill_weights(0)
                split_qk(0, 0)
                split_qk(0, 1)
                fill_weights(1)
                split_qk(1, 0)
            quads()
            power(0, LN_EPS)
            split_qk(1, 1)

            def add_bias(b):
                nc.gpsimd.tensor_tensor(x[:, b * NT:(b + 1) * NT, :], x[:, b * NT:(b + 1) * NT, :],
                                        wide[:, 1, :].unsqueeze(1).to_broadcast([P, NT, C]), ALU.add)\
                    .then_inc(x_plus, 1)

            def vblk_copy(b):
                nc.gpsimd.tensor_copy(vblk[:, :], vblk_all[:, bass.ds(b, 1), :].rearrange("p o c -> p (o c)"))\
                    .then_inc(vblk_ready, 1)

            def split_hn():
                pool.wait_ge(hnh_ready, 1)
                pool.sem_inc(hnh_ready, -1)
                split_low(hnl, hnT, hnh).then_inc(hn_split, 1)

            def add_beta(b):
                nc.gpsimd.tensor_tensor(x[:, bass.ds(b * NT, NT), :], x[:, bass.ds(b * NT, NT), :],
                                        wide[:, 4, :].unsqueeze(1).to_broadcast([P, NT, C]), ALU.add)\
                    .then_inc(beta_added, 1)

            vblk_copy(0)
            for b in range(B - 1):
                if b:
                    power(b, LN_EPS)
                pool.wait_ge(xn_copied, 1)
                pool.sem_inc(xn_copied, -1)
                add_bias(b)
            power(ROUTER, LN_EPS)
            split_hn()
            vblk_copy(1)
            add_beta(0)
            power(B - 1, LN_EPS)
            pool.wait_ge(xn_copied, 1)
            pool.sem_inc(xn_copied, -1)
            add_bias(B - 1)

            def attend_side(b, first):
                if not first:
                    vblk_copy(b + 1)
                    power(RESULT, FFN_EPS)
                power(ROUTER, LN_EPS)
                split_hn()
                add_beta(b + 1)

            attend_side(0, True)
            with pool.Fori(1, B - 1) as b:
                attend_side(b, False)
            power(RESULT, FFN_EPS)
            power(RESULT, FFN_EPS)

        @block.scalar
        def _(act):
            copy, activation = nc.scalar.copy, nc.scalar.activation

            def round_x(b):
                copy(xh[:, :], xnT_all[:, bass.ds(b * T, T)]).then_inc(xh_ready, 1)

            def from_bank(dst, src, got, read):
                act.wait_ge(got, 1)
                act.sem_inc(got, -1)
                copy(dst, src).then_inc(read, 1)

            def turned(b):
                from_bank(xnT_all[:, b * T:(b + 1) * T], bank[7][:, :], xnT_mm, xnT_read)

            def head0(b):
                act.wait_ge(h0_mm, 1)
                act.sem_inc(h0_mm, -1)
                activation(q0T[b % 2][:, :], bank[6][0:HD, :], ACT.Identity, scale=-0.125, bias=bq_neg[0:HD, 0:1])
                act.wait_ge(h0_mm, 1)
                act.sem_inc(h0_mm, -1)
                activation(k0T[b % 2][:, :], bank[7][0:HD, :], ACT.Identity, bias=b_in[0:HD, PAIRS:PAIRS + 1])\
                    .then_inc(h0_ready, 1)

            def relu(b):
                for t in range(NT):
                    if t != 1:
                        act.wait_ge(s0_mm, 1)
                        act.sem_inc(s0_mm, -1)
                    activation(tile(S0[b % 2], t), SCORE[t], ACT.Relu, scale=-1.0).then_inc(s0_relu, 1)

            def ff_out(b):
                for t in range(NT):
                    if t != 1:
                        act.wait_ge(ff_mm, 1)
                        act.sem_inc(ff_mm, -1)
                    activation(F_all[:, b * CAUSAL + QOFF[t]:b * CAUSAL + QOFF[t] + W[t]], FFOUT[t], ACT.Copy,
                               scale=-1.0).then_inc(ff_read, 1)

            def qk_part(i, pair, part):
                scale = 1.0 if part else -0.125
                bias_ = b_in[:, bass.ds(pair + PAIRS, 1)] if part else bq_neg[:, bass.ds(pair, 1)]
                act.wait_ge(qk_mm, 1)
                act.sem_inc(qk_mm, -1)
                for dst in (qk, qkh[i]):
                    activation(dst[:, part, :], bank[7][:, :], ACT.Identity, scale=scale, bias=bias_)\
                        .then_inc(lo_in, 1)

            act.wait_ge(load_w, 16 * len(LOAD_W))
            activation(bq_neg[:, :], b_in[:, 0:PAIRS], ACT.Copy, scale=-0.125).then_inc(act_own, 1)
            act.wait_ge(act_own, 1)
            act.sem_inc(act_own, -1)
            turned(0)
            head0(0)
            relu(0)
            turned(1)
            ff_out(0)
            head0(1)
            activation(kblk[:, :, :], ones[:, :].unsqueeze(1).to_broadcast([P, B, P]), ACT.Copy, scale=0.0)
            activation(vblk_all[:, :, :], ones[:, :].unsqueeze(1).to_broadcast([P, B, P]), ACT.Copy, scale=0.0)
            act.wait_ge(wide_mm, 1)
            act.sem_inc(wide_mm, -1)
            for i in range(4):
                copy(wide[:, i, :], bank[6][:, tok(i)]).then_inc(wide_read if i else wide_done, 1)
            turned(2)
            relu(1)
            head0(2)
            round_x(0)
            ff_out(1)
            turned(3)
            relu(2)
            head0(3)
            copy(wvh[:, :], w_in[:, 2 * D:3 * D]).then_inc(wv_high, 1)
            ff_out(2)
            relu(3)
            qk_part(0, 0, 0)
            ff_out(3)
            qk_part(0, 0, 1)
            copy(act_mark[:, :], b_in[:, 0:1]).then_inc(ff_ready, 1)

            def exps(s):
                for t in range(NT):
                    act.wait_ge(neg_ready, 1)
                    act.sem_inc(neg_ready, -1)
                    activation(tile(prob[s], t), tile(neg[s], t), ACT.Exp, scale=-1.0, bias=low[s][:, t:t + 1],
                               accum_out=total[s][:, t:t + 1]).then_inc(exp_done, 1)

            def probT_evac():
                for i, n in ((0, T), (2, T // 2), (1, T)):
                    act.wait_ge(tr_mm, 1)
                    act.sem_inc(tr_mm, -1)
                    copy(probT[:, i * T:i * T + n], bank[3 + i][:, 0:n]).then_inc(tr_read, 1)

            def quad(q, next_batch=None):
                for i in range(QUAD):
                    probT_evac()
                    if i % 2 == 0:
                        qk_part((i // 2 + 1) % 2, (q * 2 + 1 + i // 2) % PAIRS, 1)
                        if i == 0 and next_batch is not None:
                            round_x(next_batch)
                    else:
                        qk_part(i // 2, (q * 2 + 2 + i // 2) % PAIRS, 0)
                    exps((i + 1) % 2)

            def v_evac():
                for j in range(NT * D // T):
                    act.wait_ge(v_mm, 1)
                    act.sem_inc(v_mm, -1)
                    copy(V[:, j // 2, (j % 2) * T:(j % 2 + 1) * T], bank[3 + j % 3][:, :]).then_inc(v_read, 1)

            def projection(banks):
                for c in range(0, PAIRS, 2):
                    act.wait_ge(yT_mm_act, 1)
                    act.sem_inc(yT_mm_act, -1)
                    copy(yT[:, c, :], bank[banks[c % 4]][:, :]).then_inc(yT_read_act, 1)

            v_evac()
            qk_part(1, 1, 0)
            act.wait_ge(wide_mm, 1)
            act.sem_inc(wide_mm, -1)
            copy(wide[:, 4, :], bank[6][:, 0:C])
            copy(xkT[:, :], bank[6][:, P:P + B * XKV]).then_inc(act_own, 1)
            act.wait_ge(act_own, 1)
            act.sem_inc(act_own, -1)
            for h in range(XH):
                s = slice(h * XKV, (h + 1) * XKV)
                last = copy(kblk[s, :, s], xkT[s, :].rearrange("p (b k) -> p b k", b=B))
            last.then_inc(wide_read, 1)
            act.wait_ge(vx_mm, 1)
            act.sem_inc(vx_mm, -1)
            for h in range(XH):
                s = slice(h * XKV, (h + 1) * XKV)
                last = copy(vblk_all[s, :, s], bank[5][s, :].rearrange("p (b k) -> p b k", b=B)[:, :, s])
            last.then_inc(vx_read, 1)
            exps(0)
            with act.Fori(0, B - 1) as b:
                with act.Fori(0, QUADS - 1) as q:
                    quad(q)
                quad(QUADS - 1, b + 1)
                v_evac()
                projection(YBANKS)

            def ln_evac(bank_, dst):
                from_bank(dst, bank[bank_][:, :], ln_mm, ln_read)

            def q_evac(bank_):
                from_bank(xqT, bank[bank_][:, :], xq_mm, xq_read)

            def xs_exps():
                act.wait_ge(xs_ready, 1)
                act.sem_inc(xs_ready, -1)
                activation(xs, xs, ACT.Exp, scale=float(XHD) ** -0.5).then_inc(xs_exp, 1)

            def probs_evac(bank_):
                from_bank(xpT, bank[bank_][:, :], xp_mm, xp_read)

            def context_evac(bank_):
                from_bank(xcT, bank[bank_][:, :], xc_mm, xc_read)

            def logit_exps():
                act.wait_ge(lg_ready, 1)
                act.sem_inc(lg_ready, -1)
                activation(lg[:, :, :], lg[:, :, :], ACT.Exp).then_inc(lg_exp, 1)
                copy(hnh, hnT).then_inc(hnh_ready, 1)

            def mask_evac(bank_):
                act.wait_ge(mask_mm, 1)
                act.sem_inc(mask_mm, -1)
                copy(maskT16[:, :], bank[bank_][0:3 * E, :]).then_inc(mask_read, 1)

            with act.Fori(0, QUADS - 1) as q:
                quad(q)
            probT_evac()
            qk_part(1, PAIRS - 1, 1)
            exps(1)
            probT_evac()
            ln_evac(7, lnT[:, 0:T])
            exps(0)
            q_evac(7)
            probT_evac()
            xs_exps()
            exps(1)
            probs_evac(7)
            probT_evac()
            context_evac(7)
            projection(YBANKS_LAST)
            ln_evac(7, hnT)
            ln_evac(4, lnT[:, T:2 * T])
            ln_evac(5, lnT[:, 2 * T:3 * T])
            logit_exps()
            mask_evac(7)

            def gelus():
                for i in range(NF):
                    act.wait_ge(up_mm, 1)
                    act.sem_inc(up_mm, -1)
                    activation(interT[:, i, :], bank[2 + i][:, :], ACT.Gelu).then_inc(gelu_done, 1)

            def side(first):
                q_evac(0)
                xs_exps()
                probs_evac(6)
                context_evac(6)
                if first:
                    ln_evac(7, lnT[:, (B - 1) * T:B * T])
                ln_evac(6, hnT)
                logit_exps()
                gelus()
                mask_evac(6)

            side(True)
            with act.Fori(1, B - 1) as b:
                side(False)
            gelus()

        @block.tensor
        def _(pe):
            mm = nc.tensor.matmul

            def transposes(src, dst, ready, done):
                pe.wait_ge(ready, 1)
                pe.sem_inc(ready, -1)
                for t in range(NT):
                    last = nc.tensor.transpose(dst[:, tok(t)], src(t), ident[:, :])
                last.then_inc(done, 1)

            def turned(b):
                transposes(lambda t: xn0[:, b * NT + t, :], bank[7], xn_ready, xnT_mm)

            def head0(b):
                pe.wait_ge(xnT_read, 1)
                pe.sem_inc(xnT_read, -1)
                mm(bank[6][0:HD, :], w_in[:, 0:HD], xnT_all[:, b * T:(b + 1) * T], start=True, stop=True)\
                    .then_inc(h0_mm, 1)
                mm(bank[7][0:HD, :], w_in[:, D:D + HD], xnT_all[:, b * T:(b + 1) * T], start=True, stop=True)\
                    .then_inc(h0_mm, 1)

            def head0_scores(b):
                for t in range(NT):
                    ins = mm(SCORE[t], q0T[b % 2][:, tok(t)], k0T[b % 2][:, 0:W[t]], start=True, stop=True)
                    if t:
                        ins.then_inc(s0_mm, 1)

            def ff(b):
                for t in range(NT):
                    pe.wait_ge(s0_ready, 1)
                    pe.sem_inc(s0_ready, -1)
                    last = mm(FFOUT[t], before[:, :], tile(S0[b % 2], t), start=True, stop=(t == 0))
                    for s in range(t):
                        last = mm(FFOUT[t][:, 0:W[s]], ones[:, :], tile(S0[b % 2], s), start=False, stop=(s == t - 1))
                    if t:
                        last.then_inc(ff_mm, 1)

            def split_mm(dst, a_, b_):
                mm(dst, a_[0], b_[0], start=True, stop=False)
                mm(dst, a_[0], b_[1], start=False, stop=False)
                return mm(dst, a_[1], b_[0], start=False, stop=True)

            def project(part):
                split_mm(bank[7][:, :], (wh[:, part, :], wl[:, part, :]), (xh[:, :], xl[:, :])).then_inc(qk_mm, 1)

            def scores(i, half):
                s = slice(half * HD, (half + 1) * HD)
                for t in range(NT):
                    ins = split_mm(SCORE[t], (qkh[i][s, 0, tok(t)], qkl[i][s, 0, tok(t)]),
                                   (qkh[i][s, 1, 0:W[t]], qkl[i][s, 1, 0:W[t]]))
                    if t:
                        ins.then_inc(score_mm, 1)

            def values(head):
                for t in range(NT):
                    for k in range(t + 1):
                        last = mm(bank[6][:, t * HD:(t + 1) * HD], probT_tile(k, t),
                                  V[:, k, bass.ds(head * HD, HD)], start=(k == 0), stop=(k == t))
                last.then_inc(pv_mm, 1)

            def transpose_probs(s):
                for t in range(NT):
                    pe.wait_ge(exp_done, 1)
                    pe.sem_inc(exp_done, -1)
                    for k in range(t + 1):
                        at = KOFF[k] + (t - k) * P
                        ins = nc.tensor.transpose(bank[3 + at // T][:, at % T:at % T + P],
                                                  prob[s][:, QOFF[t] + k * P:QOFF[t] + (k + 1) * P], ident[:, :])
                        if t == NT - 1 and k != 1:
                            ins.then_inc(tr_mm, 1)

            def turn(i, head):
                transpose_probs(i % 2)
                pe.wait_ge(qk_ready, 1)
                pe.sem_inc(qk_ready, -1)
                if i % 2 == 0:
                    project(1)
                else:
                    pe.wait_ge(w_ready, 1)
                    pe.sem_inc(w_ready, -1)
                    project(0)
                scores((i + 1) % QUAD // 2, (i + 1) % 2)
                pe.wait_ge(o_free, 1)
                pe.sem_inc(o_free, -1)
                pe.wait_ge(tr_read, 3)
                pe.sem_inc(tr_read, -3)
                values(head)

            def value_projection():
                for j in range(NT * D // T):
                    if j >= 3:
                        pe.wait_ge(v_read, 1)
                        pe.sem_inc(v_read, -1)
                    t, c = j // 2, slice((j % 2) * T, (j % 2 + 1) * T)
                    split_mm(bank[3 + j % 3][:, :], (xh[:, tok(t)], xl[:, tok(t)]), (wvh[:, c], wvl[:, c]))\
                        .then_inc(v_mm, 1)

            LAST_QUAD = (QUADS - 1) * QUAD

            def yT_bank(c, banks):
                if c >= 4:
                    pe.wait_ge(yT_read_dve if c % 2 else yT_read_act, 1)
                    pe.sem_inc(yT_read_dve if c % 2 else yT_read_act, -1)
                for t in range(NT):
                    last = nc.tensor.transpose(bank[banks[c % 4]][:, tok(t)], y[:, t, c * P:(c + 1) * P], ident[:, :])
                last.then_inc(yT_mm_dve if c % 2 else yT_mm_act, 1)

            def project_tile(t):
                for c in range(PAIRS):
                    if t == 0 and c == 0:
                        pe.wait_ge(yT_read_act, 1)
                        pe.sem_inc(yT_read_act, -1)
                    if t == 0 and c > 4:
                        pe.wait_ge(yT_read_dve if c % 2 else yT_read_act, 1)
                        pe.sem_inc(yT_read_dve if c % 2 else yT_read_act, -1)
                    last = mm(bank[6][:, tok(t)], yT[:, c, tok(t)], w_proj[:, c, :], start=(c == 0),
                              stop=(c == PAIRS - 1))
                if t == NT - 1:
                    last.then_inc(proj_mm, 1)

            pe.wait_ge(const_pe, 1)
            pe.sem_inc(const_pe, -1)
            pe.wait_ge(load_w, 16 * len(LOAD_W))
            turned(0)
            head0(0)
            pe.wait_ge(h0_ready, 1)
            pe.sem_inc(h0_ready, -1)
            head0_scores(0)
            turned(1)
            ff(0)
            head0(1)
            pe.wait_ge(h0_ready, 1)
            pe.sem_inc(h0_ready, -1)
            pe.wait_ge(load_rest, REST)
            pe.wait_ge(wide_ready, 1)
            pe.sem_inc(wide_ready, -1)
            mm(bank[6][:, 0:C], ones[0:1, :], rows[:, 0, :], start=True, stop=False)
            for c in range(PAIRS):
                mm(bank[6][:, 0:C], bv_wide[:, c, :], w_proj[:, c, :], start=False, stop=(c == PAIRS - 1))
            for i in range(1, 4):
                last = mm(bank[6][:, tok(i)], ones[0:1, :], rows[:, i, :], start=True, stop=True)
            last.then_inc(wide_mm, 1)
            turned(2)
            head0_scores(1)
            pe.wait_ge(wide_read, 3)
            pe.sem_inc(wide_read, -3)
            head0(2)
            ff(1)
            pe.wait_ge(h0_ready, 1)
            pe.sem_inc(h0_ready, -1)
            turned(3)
            head0_scores(2)
            head0(3)
            ff(2)
            pe.wait_ge(h0_ready, 1)
            pe.sem_inc(h0_ready, -1)
            pe.wait_ge(w_ready, 1)
            pe.sem_inc(w_ready, -1)
            project(0)
            head0_scores(3)
            ff(3)
            pe.wait_ge(qk_ready, 1)
            pe.sem_inc(qk_ready, -1)
            project(1)
            pe.wait_ge(wv_ready, 1)
            pe.sem_inc(wv_ready, -1)
            pe.wait_ge(ff_ready, 1)
            pe.sem_inc(ff_ready, -1)
            value_projection()
            pe.wait_ge(qk_ready, 1)
            pe.sem_inc(qk_ready, -1)
            scores(0, 0)
            pe.wait_ge(w_ready, 1)
            pe.sem_inc(w_ready, -1)
            project(0)
            mm(bank[6][:, 0:C], ones[0:1, :], rows[:, 4, :], start=True, stop=True)
            mm(bank[6][:, P:P + B * XKV], xwk[:, :], ctxT[:, :, :].rearrange("p b k -> p (b k)"), start=True,
               stop=True).then_inc(wide_mm, 1)
            pe.wait_ge(v_read, 3)
            pe.sem_inc(v_read, -3)
            pe.wait_ge(ctx4_ready, 1)
            pe.sem_inc(ctx4_ready, -1)
            for b in range(B):
                last = mm(bank[5][:, tok(b)], ctx4[:, b, :, :].rearrange("p h k -> p (h k)"), xwv[:, :],
                          start=True, stop=True)
            last.then_inc(vx_mm, 1)
            pe.wait_ge(wide_read, 1)
            pe.sem_inc(wide_read, -1)
            pe.wait_ge(vx_read, 1)
            pe.sem_inc(vx_read, -1)
            with pe.Fori(0, B - 1) as b:
                with pe.Fori(0, QUADS) as q:
                    for i in range(QUAD):
                        turn(i, q * QUAD + i)
                value_projection()
                pe.wait_ge(o_free, 1)
                pe.sem_inc(o_free, -1)
                for c in range(PAIRS):
                    if 1 <= c <= 3:
                        pe.wait_ge(v_read, 1)
                        pe.sem_inc(v_read, -1)
                    yT_bank(c, YBANKS)
                for t in range(NT):
                    project_tile(t)

            def ln1(b, to):
                transposes(lambda t: xn[:, b * NT + t, :], to, xn_ready, ln_mm)

            def xq(b, to):
                mm(to[:, :], xwq[:, :], lnT[:, bass.ds(b * T, T)], start=True, stop=True).then_inc(xq_mm, 1)

            def xscore(b, to):
                for t in range(NT):
                    last = mm(to[:, tok(t)], xqT[:, tok(t)],
                              kblk[:, bass.ds(b, 1), :].rearrange("p o c -> p (o c)"), start=True, stop=True)
                last.then_inc(xs_mm, 1)

            def xprobs(b, to):
                transposes(lambda t: xs_flat[:, tok(t)], to, xp_ready, xp_mm)

            def context(b, to):
                pe.wait_ge(xp_read, 1)
                pe.sem_inc(xp_read, -1)
                pe.wait_ge(vblk_ready, 1)
                pe.sem_inc(vblk_ready, -1)
                mm(to[:, :], vblk[:, :], xpT, start=True, stop=True).then_inc(xc_mm, 1)

            def xout(b, to):
                pe.wait_ge(xc_read, 1)
                pe.sem_inc(xc_read, -1)
                for t in range(NT):
                    last = mm(to[:, tok(t)], xcT[:, tok(t)], xwo[:, :], start=True, stop=True)
                last.then_inc(xo_mm, 1)

            def ln2(b, to):
                transposes(lambda t: hn[:, t, :], to, hn_ready, ln_mm)

            def logits(b, to):
                pe.wait_ge(ln_read, 1)
                pe.sem_inc(ln_read, -1)
                for t in range(NT):
                    last = mm(to[:, t * E:(t + 1) * E], hnT[:, tok(t)], w_r[:, :], start=True, stop=True)
                last.then_inc(lg_mm, 1)

            def mask(b, to):
                pe.wait_ge(pick_ready, 1)
                pe.sem_inc(pick_ready, -1)
                for t in range(NT):
                    last = mm(to[0:3 * E, tok(t)], pick3[:, t, :], ident[:, :], start=True, stop=True)
                last.then_inc(mask_mm, 1)

            side = bank[7]
            with pe.Fori(0, QUADS - 1) as q:
                for i in range(QUAD):
                    turn(i, q * QUAD + i)
            turn(0, LAST_QUAD)
            transpose_probs(1)
            pe.wait_ge(qk_ready, 1)
            pe.sem_inc(qk_ready, -1)
            ln1(0, side)
            scores(1, 0)
            pe.wait_ge(ln_read, 1)
            pe.sem_inc(ln_read, -1)
            xq(0, side)
            pe.wait_ge(o_free, 1)
            pe.sem_inc(o_free, -1)
            pe.wait_ge(tr_read, 3)
            pe.sem_inc(tr_read, -3)
            values(LAST_QUAD + 1)
            pe.wait_ge(xq_read, 1)
            pe.sem_inc(xq_read, -1)
            xscore(0, side)
            transpose_probs(0)
            scores(1, 1)
            pe.wait_ge(o_free, 1)
            pe.sem_inc(o_free, -1)
            pe.wait_ge(tr_read, 3)
            pe.sem_inc(tr_read, -3)
            values(LAST_QUAD + 2)
            xprobs(0, side)
            transpose_probs(1)
            pe.sem_inc(last_exps, 1)
            context(0, side)
            pe.wait_ge(o_free, 1)
            pe.sem_inc(o_free, -1)
            pe.wait_ge(tr_read, 3)
            pe.sem_inc(tr_read, -3)
            values(LAST_QUAD + 3)
            xout(0, side)
            pe.wait_ge(o_free, 1)
            pe.sem_inc(o_free, -1)
            yT_bank(0, YBANKS_LAST)
            yT_bank(1, YBANKS_LAST)
            for c in range(2, PAIRS):
                yT_bank(c, YBANKS_LAST)
            project_tile(0)
            ln2(0, side)
            ln1(1, bank[4])
            ln1(2, bank[5])
            project_tile(1)
            logits(0, side)
            pe.wait_ge(ln_read, 2)
            pe.sem_inc(ln_read, -2)
            project_tile(2)
            project_tile(3)
            mask(0, side)
            pe.wait_ge(o_free, 1)
            pe.sem_inc(o_free, -1)

            def spread_mask(e):
                mm(bank[e % 2][:, :], sel16[:, e, :], maskT16[0:E, :], start=True, stop=True).then_inc(bc_mm, 1)

            def experts_start():
                pe.wait_ge(mask_read, 1)
                pe.sem_inc(mask_read, -1)
                spread_mask(0)
                spread_mask(1)
                for i in range(NF):
                    mm(bank[2 + i][:, :], b1_parts[:, tok(i)], maskT16[:, :], start=True, stop=False)

            MASK_AT = {NF * (e - 2): e for e in range(2, E)}
            STEP_AT = {7: xprobs, 9: context, 11: xout, 21: ln2, 23: logits}

            def experts(steps, b):
                for n in range(E * NF):
                    e, i = divmod(n, NF)
                    if n in MASK_AT:
                        pe.wait_ge(xm_ready, 1)
                        pe.sem_inc(xm_ready, -1)
                        spread_mask(MASK_AT[n])
                    if i == 0 and e >= E - 2:
                        pe.wait_ge(xm_ready, 1)
                        pe.sem_inc(xm_ready, -1)
                    x_ = xm[e % 3]
                    mm(bank[2 + i][:, :], w1h[:, e, tok(i)], x_[:, 0, :], start=False, stop=False)
                    mm(bank[2 + i][:, :], w1h[:, e, tok(i)], x_[:, 1, :], start=False, stop=False)
                    ins = mm(bank[2 + i][:, :], w1l[:, e, tok(i)], x_[:, 0, :], start=False, stop=(e == E - 1))
                    if e == E - 1:
                        ins.then_inc(up_mm, 1)
                    if n in steps:
                        steps[n](b, bank[6])

            def down():
                for i in range(NF):
                    pe.wait_ge(gelu_done, 1)
                    pe.sem_inc(gelu_done, -1)
                    for t in range(NT):
                        last = mm(bank[7][:, tok(t)], interT[:, i, tok(t)], w2[:, i, :], start=(i == 0 and t == 0),
                                  stop=(i == NF - 1 and t == NT - 1))
                last.then_inc(down_mm, 1)

            def last_ln1(b, to):
                ln1(B - 1, bank[7])

            def last_ln1_read(b, to):
                pe.wait_ge(ln_read, 1)
                pe.sem_inc(ln_read, -1)

            def feed_forward(b, first):
                xq(b + 1, bank[0])
                if not first:
                    down()
                pe.wait_ge(xq_read, 1)
                pe.sem_inc(xq_read, -1)
                experts_start()
                xscore(b + 1, bank[6])
                experts({**STEP_AT, 16: last_ln1, 18: last_ln1_read} if first else STEP_AT, b + 1)
                mask(b + 1, bank[6])

            feed_forward(0, True)
            with pe.Fori(1, B - 1) as b:
                feed_forward(b, False)
            down()
            experts_start()
            experts({}, None)
            down()

        @block.vector
        def _(dve):
            v = nc.vector

            def own(ins):
                ins.then_inc(dve_own, 1)
                dve.wait_ge(dve_own, 1)
                dve.sem_inc(dve_own, -1)

            def moments(src, slot):
                for t in range(NT):
                    last = v.bn_stats(stats[:, slot * NT + t, :], src(t))
                own(last)
                for t in range(NT):
                    last = v.bn_aggr(mv[:, slot, t, :], stats[:, slot * NT + t, :])
                last.then_inc(var_ready, 1)

            def normalise(src, slot, dst):
                dve.wait_ge(rstd_ready, 1)
                dve.sem_inc(rstd_ready, -1)
                for t in range(NT):
                    last = v.tensor_scalar(dst(t), src(t), mv[:, slot, t, 0:1], rstd[:, slot, t:t + 1], ALU.subtract,
                                           ALU.mult)
                return last

            for b in range(B):
                if b == 0:
                    dve.wait_ge(load_x0, 16)
                if b == 1:
                    dve.wait_ge(load_x, 16 * (B - 1))
                moments(lambda t: x[:, b * NT + t, :], b)
                if b == 0:
                    normalise(lambda t: x[:, t, :], 0, lambda t: xn0[:, t, :]).then_inc(xn_ready, 1)
            for b in range(1, B):
                normalise(lambda t: x[:, b * NT + t, :], b, lambda t: xn0[:, b * NT + t, :]).then_inc(xn_ready, 1)
            dve.wait_ge(const_dve, 1)
            dve.sem_inc(const_dve, -1)
            dve.wait_ge(load_w, 16 * len(LOAD_W))
            for c in range(PAIRS):
                last = v.tensor_scalar(bv_wide[:, c, :], ones[:, :], b_in[:, 2 * PAIRS + c:2 * PAIRS + c + 1], None,
                                       ALU.mult)
            last.then_inc(wide_ready, 1)
            dve.wait_ge(load_rest, REST)
            for h in range(XH):
                last = v.tensor_copy(ctx4[:, :, h, :], ctxT[:, :, :])
            last.then_inc(ctx4_ready, 1)

            def prune_round(tiles_=range(NT), again=True):
                for t in tiles_:
                    if again:
                        dve.wait_ge(pick_own[t], 1)
                        dve.sem_inc(pick_own[t], -1)
                    row = work[:, WOFF[t]:WOFF[t] + PADS + W[t]]
                    v.max(best[:, t, :], row).then_inc(pick_own[t], 1)
                for t in tiles_:
                    row = work[:, WOFF[t]:WOFF[t] + PADS + W[t]]
                    dve.wait_ge(pick_own[t], 1)
                    dve.sem_inc(pick_own[t], -1)
                    v.match_replace(row, best[:, t, :], row, MARK).then_inc(pick_own[t], 1)

            def prune_wait(tiles_=range(NT)):
                for t in tiles_:
                    dve.wait_ge(pick_own[t], 1)
                    dve.sem_inc(pick_own[t], -1)

            def fill_work(b, tiles_=range(NT), first=False):
                for t in tiles_:
                    v.memset(work[:, WOFF[t]:WOFF[t] + PADS], PAD)
                    if first:
                        dve.wait_ge(F_ready, 1)
                        dve.sem_inc(F_ready, -1)
                    last = v.tensor_copy(work_row(t), F_all[:, bass.ds(b * CAUSAL + QOFF[t], W[t])])
                own(last)

            def mark_dropped(tiles_=range(NT)):
                for t in tiles_:
                    row = work_row(t)
                    if t:
                        v.tensor_scalar(row[:, 0:t * P], row[:, 0:t * P], -PAD, BIG, ALU.is_gt, ALU.mult)
                    last = v.scalar_tensor_tensor(out=row[:, t * P:W[t]], in0=row[:, t * P:W[t]], scalar=-PAD,
                                                  in1=drop[:, :], op0=ALU.is_gt, op1=ALU.mult)
                return last

            def add_ff(b, dst, tiles_=range(NT)):
                for t in tiles_:
                    last = v.tensor_tensor(dst(t), work_row(t), F_all[:, bass.ds(b * CAUSAL + QOFF[t], W[t])],
                                           ALU.subtract)
                return last

            def set_bias():
                for t in range(NT):
                    last = v.tensor_copy(tile(bias, t), work_row(t))
                own(last)

            def biased(s):
                for t in range(NT):
                    if t != 1:
                        dve.wait_ge(score_mm, 1)
                        dve.sem_inc(score_mm, -1)
                    v.tensor_tensor_reduce(out=tile(neg[s], t), in0=SCORE[t], in1=tile(bias, t), scale=1.0,
                                           scalar=3.0e38, op0=ALU.add, op1=ALU.min,
                                           accum_out=low[s][:, t:t + 1]).then_inc(neg_ready, 1)

            def invert(s):
                v.reciprocal(inv[s][:, :], total[s][:, :]).then_inc(inv_ready, 1)

            def head_out(s, head):
                dve.wait_ge(inv_ready, 1)
                dve.sem_inc(inv_ready, -1)
                dve.wait_ge(pv_mm, 1)
                dve.sem_inc(pv_mm, -1)
                v.tensor_tensor(y[:, :, bass.ds(head * HD, HD)],
                                bank[6][:, 0:NT * HD].rearrange("p (t d) -> p t d", t=NT),
                                inv[s][:, :].unsqueeze(2).to_broadcast([P, NT, HD]), ALU.mult).then_inc(o_free, 1)

            def yT_evac(c, banks):
                dve.wait_ge(yT_mm_dve, 1)
                dve.sem_inc(yT_mm_dve, -1)
                v.tensor_copy(yT[:, c, :], bank[banks[c % 4]][:, :]).then_inc(yT_read_dve, 1)

            def projection_add(b):
                dve.wait_ge(proj_mm, 1)
                dve.sem_inc(proj_mm, -1)
                rows_b = x[:, bass.ds(b * NT, NT), :]
                return v.tensor_tensor(rows_b, bank[6][:, :].rearrange("p (t c) -> p t c", t=NT), rows_b, ALU.add)

            dve.sem_inc(o_free, 1)
            UNROLL = 4
            assert (ROUNDS - 1) % UNROLL == 0
            for two in (range(0, 2), range(2, NT)):
                fill_work(0, two, True)
                prune_round(two, False)
                with dve.Fori(0, (ROUNDS - 1) // UNROLL) as n:
                    for _ in range(UNROLL):
                        prune_round(two)
                prune_wait(two)
                own(mark_dropped(two))
                own(add_ff(0, lambda t: tile(bias, t), two))
            biased(0)
            dve.wait_ge(F_ready, B * NT - NT)
            dve.sem_inc(F_ready, -(B * NT - NT))
            fill_work(1)

            with dve.Fori(0, B - 1) as b:
                prune_round(again=False)
                with dve.Fori(0, QUADS - 1) as q:
                    for i in range(QUAD):
                        biased((i + 1) % 2)
                        invert(i % 2)
                        prune_round()
                        head_out(i % 2, q * QUAD + i)
                biased(1)
                invert(0)
                prune_wait()
                own(mark_dropped())
                head_out(0, H - 4)
                biased(0)
                invert(1)
                own(add_ff(b + 1, work_row))
                head_out(1, H - 3)
                biased(1)
                invert(0)
                own(v.memset(mark[:, 0:1], 0.0))
                set_bias()
                head_out(0, H - 2)
                biased(0)
                invert(1)
                head_out(1, H - 1)
                for c in range(1, PAIRS, 2):
                    yT_evac(c, YBANKS)
                fill_work((b + 2) % B)
                projection_add(b).then_inc(o_free, 1)

            def wide4(i):
                return wide[:, i, :].unsqueeze(1).to_broadcast([P, NT, C])

            def tiles(buf):
                return buf[:, :].rearrange("p (t c) -> p t c", t=NT)

            def rows_of(b):
                return x[:, bass.ds(b * NT, NT), :]

            def row_of(b):
                return lambda t: x[:, bass.ds(b * NT + t, 1), :].rearrange("p o c -> p (o c)")

            def attend_norm(b):
                normalise(row_of(b), b, lambda t: xn[:, b * NT + t, :]).then_inc(xn_ready, 1)
                v.memset(mark[:, 1 + b:2 + b], 0.0).then_inc(xn_copied, 1)

            def xs_minus_max(side):
                dve.wait_ge(xs_mm, 1)
                dve.sem_inc(xs_mm, -1)
                xs_bank = side[:, :].rearrange("p (g k) -> p g k", k=XKV)
                own(v.tensor_reduce(xmax[:, :], xs_bank, AX.X, ALU.max))
                v.tensor_tensor(xs, xs_bank, xmax[:, :].unsqueeze(2).to_broadcast([P, NT * XH, XKV]),
                                ALU.subtract).then_inc(xs_ready, 1)

            def xs_divide():
                dve.wait_ge(xs_exp, 1)
                dve.sem_inc(xs_exp, -1)
                own(v.tensor_reduce(xsum[:, :], xs, AX.X, ALU.add))
                own(v.reciprocal(xsum[:, :], xsum[:, :]))
                v.tensor_tensor(xs, xs, xsum[:, :].unsqueeze(2).to_broadcast([P, NT * XH, XKV]),
                                ALU.mult).then_inc(xp_ready, 1)

            def attend_add(b, side):
                dve.wait_ge(xo_mm, 1)
                dve.sem_inc(xo_mm, -1)
                dve.wait_ge(x_plus, 1)
                dve.sem_inc(x_plus, -1)
                own(v.tensor_tensor(rows_of(b), tiles(side), rows_of(b), ALU.add))
                moments(row_of(b), ROUTER)

            def route_norm(b):
                normalise(row_of(b), ROUTER, lambda t: hn[:, t, :]).then_inc(hn_ready, 1)

            def each(buf):
                return buf[:, :].unsqueeze(2).to_broadcast([P, NT, E])

            def route(side):
                dve.wait_ge(lg_mm, 1)
                dve.sem_inc(lg_mm, -1)
                lg_bank = side[:, 0:NT * E].rearrange("p (t e) -> p t e", t=NT)
                own(v.tensor_reduce(lmax[:, :], lg_bank, AX.X, ALU.max))
                v.tensor_tensor(lg[:, :, :], lg_bank, each(lmax), ALU.subtract).then_inc(lg_ready, 1)
                dve.wait_ge(lg_exp, 1)
                dve.sem_inc(lg_exp, -1)
                own(v.tensor_reduce(lsum[:, :], lg[:, :, :], AX.X, ALU.add))
                own(v.reciprocal(lsum[:, :], lsum[:, :]))
                own(v.tensor_tensor(lg[:, :, :], lg[:, :, :], each(lsum), ALU.mult))
                own(v.tensor_reduce(lmax[:, :], lg[:, :, :], AX.X, ALU.max))
                own(v.tensor_tensor(pick[:, :, :], lg[:, :, :], each(lmax), ALU.is_equal))
                own(v.tensor_tensor(pick[:, :, :], pick[:, :, :], rank[:, :, :], ALU.mult))
                own(v.tensor_reduce(lmax[:, :], pick[:, :, :], AX.X, ALU.max))
                for i in range(3):
                    last = v.tensor_tensor(pick3[:, :, i * E:(i + 1) * E], pick[:, :, :], each(lmax), ALU.is_equal)
                last.then_inc(pick_ready, 1)

            def expert_inputs(lo, hi):
                for e in range(lo, hi):
                    dve.wait_ge(bc_mm, 1)
                    dve.sem_inc(bc_mm, -1)
                    v.tensor_tensor(xm[e % 3][:, 0, :], bank[e % 2][:, :], hnh.bitcast(F32), ALU.mult)
                    v.tensor_tensor(xm[e % 3][:, 1, :], bank[e % 2][:, :], hnl.bitcast(F32), ALU.mult)\
                        .then_inc(xm_ready, 1)

            def start_result():
                dve.wait_ge(res_free, 1)
                dve.sem_inc(res_free, -1)
                own(v.tensor_tensor(res[:, :, :], hn, wide4(2), ALU.add))

            def down_out():
                dve.wait_ge(down_mm, 1)
                dve.sem_inc(down_mm, -1)
                own(v.tensor_tensor(res[:, :, :], tiles(bank[7]), res[:, :, :], ALU.add))

            def split_w1(e):
                whole = w1[:, bass.ds(e, 1), :].rearrange("p o f -> p (o f)")
                own(v.tensor_copy(w1_high, whole))
                own(v.tensor_tensor(w1l[:, bass.ds(e, 1), :].rearrange("p o f -> p (o f)"), whole,
                                    w1_high.bitcast(F32), ALU.subtract))
                own(v.tensor_copy(w1h[:, bass.ds(e, 1), :].rearrange("p o f -> p (o f)"), w1_high.bitcast(F32)))

            moments(row_of(0), 0)
            with dve.Fori(0, E // QUAD) as q:
                for i in range(QUAD):
                    biased((i + 1) % 2)
                    invert(i % 2)
                    head_out(i % 2, q * QUAD + i)
                    split_w1(q * QUAD + i)
            with dve.Fori(E // QUAD, QUADS - 1) as q:
                for i in range(QUAD):
                    biased((i + 1) % 2)
                    invert(i % 2)
                    head_out(i % 2, q * QUAD + i)
            biased(1)
            invert(0)
            attend_norm(0)
            head_out(0, H - 4)
            biased(0)
            invert(1)
            moments(row_of(1), 1)
            head_out(1, H - 3)
            xs_minus_max(bank[7])
            biased(1)
            invert(0)
            xs_divide()
            head_out(0, H - 2)
            attend_norm(1)
            moments(row_of(2), 2)
            dve.wait_ge(last_exps, 1)
            dve.sem_inc(last_exps, -1)
            invert(1)
            attend_norm(2)
            head_out(1, H - 1)
            yT_evac(1, YBANKS_LAST)
            yT_evac(3, YBANKS_LAST)
            attend_add(0, bank[7])
            yT_evac(5, YBANKS_LAST)
            yT_evac(7, YBANKS_LAST)
            route_norm(0)
            route(bank[7])
            own(projection_add(B - 1))
            dve.sem_inc(o_free, 1)
            def result_moments():
                moments(lambda t: res[:, t, :], RESULT)
                own(v.memset(mark[:, 0:1], 0.0))

            def result(rows_b):
                for t in range(NT):
                    last = v.scalar_tensor_tensor(out=res[:, t, :], in0=res[:, t, :], scalar=mv[:, RESULT, t, 0:1],
                                                  in1=wide[:, 3, :], op0=ALU.subtract, op1=ALU.mult)
                own(last)
                dve.wait_ge(rstd_ready, 1)
                dve.sem_inc(rstd_ready, -1)
                dve.wait_ge(beta_added, 1)
                dve.sem_inc(beta_added, -1)
                for t in range(NT):
                    last = v.scalar_tensor_tensor(out=res[:, t, :], in0=res[:, t, :],
                                                  scalar=rstd[:, RESULT, t:t + 1], in1=rows_b(t), op0=ALU.mult,
                                                  op1=ALU.add)
                last.then_inc(res_ready, 1)

            def feed_forward(b, first):
                dve.wait_ge(hn_split, 1)
                dve.sem_inc(hn_split, -1)
                expert_inputs(0, 1)
                if not first:
                    down_out()
                xs_minus_max(bank[6])
                expert_inputs(1, 3)
                xs_divide()
                if first:
                    moments(row_of(B - 1), B - 1)
                else:
                    result_moments()
                expert_inputs(3, 4)
                if first:
                    attend_norm(B - 1)
                else:
                    result(row_of(b - 1))
                expert_inputs(4, 5)
                attend_add(b + 1, bank[6])
                expert_inputs(5, 6)
                start_result()
                route_norm(b + 1)
                expert_inputs(6, 8)
                route(bank[6])

            feed_forward(0, True)
            with dve.Fori(1, B - 1) as b:
                feed_forward(b, False)
            dve.wait_ge(hn_split, 1)
            dve.sem_inc(hn_split, -1)
            expert_inputs(0, 1)
            down_out()
            expert_inputs(1, 3)
            result_moments()
            expert_inputs(3, 4)
            result(row_of(B - 2))
            expert_inputs(4, E)
            start_result()
            down_out()
            result_moments()
            result(row_of(B - 1))


_SHAPES = {"x": (P, B * NT, C), "w_in": (C, 3 * D), "b_in": (P, 3 * PAIRS), "w_proj": (P, PAIRS, C), "xwq": (C, C),
           "xwk": (CD, C), "xwv": (CD, C), "xwo": (C, C), "ctxT": (CD, B, XKV), "w_r": (C, E), "w1": (C, E, FF),
           "b1": (E, FF), "w2": (P, NF, C), "rows": (1, 5, C)}


def kernel(**inputs):
    import numpy as np
    import concourse.bacc as bacc
    from concourse.bass_utils import run_bass_kernel_spmd

    i = {k: np.asarray(v) for k, v in inputs.items()}
    laid = {
        "x": i["x"].reshape(B * NT, P, C).transpose(1, 0, 2),
        "w_in": i["L0_attn_W_attn"].T,
        "b_in": i["L0_attn_b_attn"].reshape(3 * PAIRS, P).T,
        "w_proj": i["L0_attn_W_proj"].T.reshape(PAIRS, P, C).transpose(1, 0, 2),
        "xwq": i["L0_xattn_Wq"].T,
        "xwk": i["L0_xattn_Wk"].T,
        "xwv": i["L0_xattn_Wv"].T,
        "xwo": i["L0_xattn_Wo"].T,
        "ctxT": i["ctx_768"].transpose(2, 0, 1),
        "w_r": i["L0_ffn_Wr"].T,
        "w1": i["L0_ffn_W1"].transpose(1, 0, 2),
        "b1": i["L0_ffn_b1"],
        "w2": i["L0_ffn_Wo"].reshape(NF, P, C).transpose(1, 0, 2),
        "rows": np.stack([i["L0_attn_b_proj"], i["L0_xattn_bo"], i["L0_ffn_bo"], i["L0_ffn_gamma"],
                          i["L0_ffn_beta"]])[None],
    }
    nc = bacc.Bacc("TRN2", target_bir_lowering=False, num_devices=1)
    handles = {n: nc.dram_tensor(f"in_{n}", s, F32, kind="ExternalInput").ap() for n, s in _SHAPES.items()}
    out = nc.dram_tensor("out_0", (B, T, C), F32, kind="ExternalOutput").ap()
    program(nc, handles, out)
    launched = run_bass_kernel_spmd(
        nc, [{f"in_{n}": np.ascontiguousarray(laid[n]) for n in _SHAPES}], core_ids=[0])
    return launched.results[0]["out_0"]
```
